# Optimizing a Trainium2 kernel written in Bass

```python
import numpy as np
import jax
import jax.numpy as jnp

def _softmax(x, axis=-1):
    return jax.nn.softmax(x, axis=axis)

def _gelu(x):
    return jax.nn.gelu(x, approximate=True)

def _silu(x):
    return jax.nn.silu(x)

def _sigmoid(x):
    return jax.nn.sigmoid(x)

def _layernorm(x, axis=-1, eps=1e-05):
    m = jnp.mean(x, axis=axis, keepdims=True)
    v = jnp.var(x, axis=axis, keepdims=True)
    return (x - m) / jnp.sqrt(v + eps)

def _scatter_add(tgt, idx, src, axis=0):
    return tgt.at[idx].add(src)

def _segment_sum(src, seg, n):
    return jax.ops.segment_sum(src, seg, n)
kernel_name = 'mk_early_fusion_d1_tok_img768_r4_190628'

def setup_inputs(seed: int=0):
    np.random.seed(seed)
    _w = jnp.asarray

    def _rec_inputs():
        import jax
        import jax.numpy as jnp
        _rk = jax.random.key(seed)
        x = -0.000356955 + 1 * jax.random.normal(jax.random.fold_in(_rk, 1), (16, 3, 224, 224), jnp.float32)
        txt = 0.000668493 + 0.999545 * jax.random.normal(jax.random.fold_in(_rk, 2), (16, 128, 192), jnp.float32)
        return (x, txt)
    x, txt = _rec_inputs()

    def _L0_tok_setup():
        import jax, jax.numpy as jnp
        import numpy as np
        IMG = 224
        P = 16
        C = 3
        E = 192
        B = 128
        GH = IMG // P
        N = GH * GH
        key = jax.random.key(seed)
        kx, kw, kb = jax.random.split(key, 3)
        x = jax.random.normal(kx, (B, C, IMG, IMG), dtype=jnp.float32)
        W = jax.random.normal(kw, (E, C, P, P), dtype=jnp.float32) * (1.0 / np.sqrt(C * P * P))
        b = jnp.zeros((E,), dtype=jnp.float32)
        return {'x': x, 'W': W, 'b': b}
    _L0_tok_all = _L0_tok_setup()
    _L0_tok_in = {k: v for k, v in _L0_tok_all.items() if k in ('W', 'b')}
    del _L0_tok_all

    def _L0_attn_setup():
        import jax, jax.numpy as jnp
        import numpy as np
        B, S, D, H = (64, 577, 192, 12)
        DH = D // H
        key = jax.random.key(seed)
        ks = jax.random.split(key, 9)
        sc = 0.02
        return {'x': jax.random.normal(ks[0], (B, S, D), jnp.float32), 'Wq': jax.random.normal(ks[1], (H, D, DH), jnp.float32) * sc, 'bq': jnp.zeros((H, DH), jnp.float32), 'Wk': jax.random.normal(ks[2], (H, D, DH), jnp.float32) * sc, 'bk': jnp.zeros((H, DH), jnp.float32), 'Wv': jax.random.normal(ks[3], (H, D, DH), jnp.float32) * sc, 'bv': jnp.zeros((H, DH), jnp.float32), 'Wo': jax.random.normal(ks[4], (D, D), jnp.float32) * sc, 'bo': jnp.zeros((D,), jnp.float32)}
    _L0_attn_all = _L0_attn_setup()
    _L0_attn_in = {k: v for k, v in _L0_attn_all.items() if k in ('Wq', 'bq', 'Wk', 'bk', 'Wv', 'bv', 'Wo', 'bo')}
    del _L0_attn_all

    def _L0_ffn_setup():
        import jax, jax.numpy as jnp
        import numpy as np
        E, C, F, K = (8, 192, 768, 2)
        key = jax.random.key(seed)
        k0, k1, k2, k3 = jax.random.split(key, 4)
        B, T = (8, 512)
        return {'x': jax.random.normal(k0, (B, T, C), jnp.float32), 'router_w': jax.random.normal(k1, (E, C), jnp.float32) * 0.02, 'w1': jax.random.normal(k2, (E, C, F), jnp.float32) * 0.02, 'b1': jnp.zeros((E, F), jnp.float32), 'w2': jax.random.normal(k3, (E, F, C), jnp.float32) * 0.02, 'b2': jnp.zeros((E, C), jnp.float32)}
    _L0_ffn_all = _L0_ffn_setup()
    _L0_ffn_in = {k: v for k, v in _L0_ffn_all.items() if k in ('router_w', 'w1', 'b1', 'w2', 'b2')}
    del _L0_ffn_all
    return {'x': x, 'txt': txt, 'L0_tok_W': _L0_tok_in['W'], 'L0_tok_b': _L0_tok_in['b'], 'L0_attn_Wq': _L0_attn_in['Wq'], 'L0_attn_bq': _L0_attn_in['bq'], 'L0_attn_Wk': _L0_attn_in['Wk'], 'L0_attn_bk': _L0_attn_in['bk'], 'L0_attn_Wv': _L0_attn_in['Wv'], 'L0_attn_bv': _L0_attn_in['bv'], 'L0_attn_Wo': _L0_attn_in['Wo'], 'L0_attn_bo': _L0_attn_in['bo'], 'L0_ffn_router_w': _L0_ffn_in['router_w'], 'L0_ffn_w1': _L0_ffn_in['w1'], 'L0_ffn_b1': _L0_ffn_in['b1'], 'L0_ffn_w2': _L0_ffn_in['w2'], 'L0_ffn_b2': _L0_ffn_in['b2']}

def reference(x, txt, L0_tok_W, L0_tok_b, L0_attn_Wq, L0_attn_bq, L0_attn_Wk, L0_attn_bk, L0_attn_Wv, L0_attn_bv, L0_attn_Wo, L0_attn_bo, L0_ffn_router_w, L0_ffn_w1, L0_ffn_b1, L0_ffn_w2, L0_ffn_b2):
    import jax
    import jax.numpy as jnp

    def _L0_tok_ref(x, W, b):
        import jax, jax.numpy as jnp
        import numpy as np
        IMG = 224
        P = 16
        C = 3
        E = 192
        B = 128
        GH = IMG // P
        N = GH * GH
        Bn = x.shape[0]
        patches = x.reshape(Bn, C, GH, P, GH, P).transpose(0, 2, 4, 1, 3, 5).reshape(Bn, N, C * P * P)
        Wm = W.reshape(E, C * P * P)
        out = jnp.einsum('bnk,ek->bne', patches, Wm) + b
        return out

    def _L0_attn_ref(x, Wq, bq, Wk, bk, Wv, bv, Wo, bo):
        import jax, jax.numpy as jnp
        import numpy as np
        B, S, D, H = (64, 577, 192, 12)
        DH = D // H
        q = jnp.einsum('bsd,hde->bhse', x, Wq) + bq[None, :, None, :]
        k = jnp.einsum('bsd,hde->bhse', x, Wk) + bk[None, :, None, :]
        v = jnp.einsum('bsd,hde->bhse', x, Wv) + bv[None, :, None, :]
        scale = np.float32(1.0 / np.sqrt(DH))
        scores = jnp.einsum('bhqe,bhke->bhqk', q, k) * scale
        probs = jax.nn.softmax(scores, axis=2)
        ctx = jnp.einsum('bhqk,bhke->bhqe', probs, v)
        ctx = ctx.transpose(0, 2, 1, 3).reshape(x.shape[0], x.shape[1], H * DH)
        return ctx @ Wo + bo

    def _L0_ffn_ref(x, router_w, w1, b1, w2, b2):
        import jax, jax.numpy as jnp
        import numpy as np
        E, C, F, K = (8, 192, 768, 2)
        B, T, Cc = x.shape
        flat = x.reshape(-1, Cc)
        logits = flat @ router_w.T
        probs = jax.nn.softmax(logits.astype(jnp.float32), axis=-1)
        top_w, top_i = jax.lax.top_k(probs, K)
        top_w = (top_w / top_w.sum(-1, keepdims=True)).astype(x.dtype)
        out = jnp.zeros_like(flat)
        for e in range(E):
            w_e = jnp.sum(top_w * (top_i == e), axis=-1)[:, None]
            h = jax.nn.gelu(flat @ w1[e] + b1[e], approximate=False)
            out = out + w_e * (h @ w2[e] + b2[e])
        return out.reshape(B, T, Cc)
    h = _L0_tok_ref(x, L0_tok_W, L0_tok_b)
    h = jnp.concatenate([h, txt], axis=1)
    h = h + _L0_attn_ref(_layernorm(h, axis=-1), L0_attn_Wq, L0_attn_bq, L0_attn_Wk, L0_attn_bk, L0_attn_Wv, L0_attn_bv, L0_attn_Wo, L0_attn_bo)
    h = h + _L0_ffn_ref(_layernorm(h, axis=-1), L0_ffn_router_w, L0_ffn_w1, L0_ffn_b1, L0_ffn_w2, L0_ffn_b2)
    return h

_drawn_inputs = setup_inputs


def setup_inputs(seed=0):
    import zlib

    import numpy as np

    out = dict(_drawn_inputs(seed))
    spreads = {'L0_tok_b': (0.0, 0.1),
     'L0_attn_bq': (0.0, 0.8),
     'L0_attn_bk': (0.0, 0.8),
     'L0_attn_bv': (0.0, 0.1),
     'L0_attn_bo': (0.0, 0.1),
     'L0_ffn_b1': (0.0, 0.376),
     'L0_ffn_b2': (0.0, 0.1)}
    factors = {'L0_attn_Wq': 8.0, 'L0_attn_Wk': 8.0, 'L0_attn_Wv': 7.127}
    for name, (base, spread) in spreads.items():
        noise = np.random.default_rng([zlib.crc32(name.encode()), seed]).standard_normal(out[name].shape)
        drawn = base * np.exp(spread * noise) if base else spread * noise
        out[name] = jnp.asarray(drawn.astype(out[name].dtype))
    for name, factor in factors.items():
        out[name] = (out[name] * factor).astype(out[name].dtype)
    return out
```

```python
import concourse.bass as bass
from concourse import mybir
from contextlib import ExitStack

F32 = mybir.dt.float32
BF16 = mybir.dt.bfloat16
I32 = mybir.dt.int32
ALU = mybir.AluOpType
ACT = mybir.ActivationFunctionType
AX = mybir.AxisListType

E, TOPK = 8, 2
H, DH = 12, 16
D = H * DH
DC = D // 2
F = 768
FC = F // 128
C, P, GRID = 3, 16, 14
KTOK = C * P * P
KC = KTOK // 128
NPATCH, NTEXT = GRID * GRID, 128
S = NPATCH + NTEXT
SC, SQ = 3, 108
HALF = H // 2
EPS = 1e-5
YWORDS = 3 * D // 2
TOKEN = YWORDS + E
XROW = TOKEN + 1
STACK_Q = ((0, 0, 3), (1, 48, 2), (2, 80, 1))
STACK_K = ((0, 0, 3), (0, 48, 2), (0, 80, 1))
PLACE = 4
ROUTE = 14
W1CHUNK = (0, 1, 2, 0, 1)


class Step:

    def __init__(self, turn, k, of):
        self.of, self.turn, self.slot = of, turn + k // of, k % of
        self.odd = self.slot % 2
        self.i = of * self.turn + self.slot

    def __add__(self, n):
        return Step(self.turn, self.slot + n, self.of)


def wait(eng, sem, value):
    if not (isinstance(value, int) and value <= 0):
        eng.wait_ge(sem, value)


def settle(eng, settled):
    eng.sem_inc(settled, 1)


def fusion_layer(nc, x, txt, tok_w, tok_b, wq, bq, wk, bk, wv, bv, wo, bo, router, w1, b1, w2, b2, out):
    B = x.shape[0]
    NTOK = B * S
    REGION = NTOK + 128
    NTILE = (TOPK * NTOK + E * 127) // 128
    NSPARE = E
    GB = 8
    NG = B // GB
    NCONST = 3 + H + 1 + 2 + 1
    GR = GB * GRID

    patch_rows = nc.dram_tensor("patch_rows", [B * NPATCH, D], F32, kind="Internal").ap()
    qk_parts = nc.dram_tensor("qk_parts", [2, 4, 3 * DC, S], BF16, kind="Internal").ap()
    expert_rows = nc.dram_tensor("expert_rows", [E * REGION + NSPARE * 128, XROW], I32, kind="Internal").ap()

    top = ExitStack()
    with top:
        def sem(name):
            return top.enter_context(nc.semaphore(name))

        def sb(stack, name, shape, dt=F32):
            return stack.enter_context(nc.sbuf_tensor(name, shape, dt))

        bank = [top.enter_context(nc.psum_tensor(f"bank{n}", [128, 512], F32)) for n in range(8)]

        w1_parts = sb(top, "w1_parts", [128, E, 3, F], BF16)
        w2_hi = sb(top, "w2_hi", [128, E, FC, D], BF16)
        w2_lo = sb(top, "w2_lo", [128, E, FC, D], BF16)
        b1_cols = sb(top, "b1_cols", [128, E * FC])
        b2_rows = sb(top, "b2_rows", [128, E, D])
        ident = sb(top, "ident", [128, 128])
        ident_h = sb(top, "ident_h", [128, 128], BF16)
        pad_row = sb(top, "pad_row", [128, XROW], I32)
        carry = sb(top, "carry", [128, E])
        lanes = sb(top, "lanes", [128, 1])
        lanes_i = sb(top, "lanes_i", [128, 1], I32)
        tile_row = sb(top, "tile_row", [1, NTILE], I32)
        tile_expert = sb(top, "tile_expert", [1, NTILE], I32)
        tile_land = sb(top, "tile_land", [1, 4, NTILE], I32)
        land = sb(top, "land", [1, NTILE], I32)

        count = sb(top, "count", [1, E])
        count_i = sb(top, "count_i", [1, E], I32)
        tiles = sb(top, "tiles", [1, E])
        ends = sb(top, "ends", [1, E])
        tile_no = sb(top, "tile_no", [1, NTILE])
        tile_no_i = sb(top, "tile_no_i", [1, NTILE], I32)
        owner = sb(top, "owner", [1, NTILE])
        begun = sb(top, "begun", [1, NTILE])
        step_no = sb(top, "step_no", [1, NTILE])
        base = sb(top, "base", [1, NTILE])
        spare = sb(top, "spare", [1, NTILE])
        pad_at = sb(top, "pad_at", [128, E], I32)


        made = sem("made")
        pool_settled, dve_settled = sem("pool_settled"), sem("dve_settled")
        pe_settled, sp_settled = sem("pe_settled"), sem("sp_settled")
        made_v = sem("made_v")
        image_in = [sem(f"image_in{g}") for g in range(NG)]
        tokw_in = sem("tokw_in")
        tokw_t = sem("tokw_t")
        tokw_copied = sem("tokw_copied")
        strip_t = sem("strip_t")
        strip_copied_v = sem("strip_copied_v")
        strip_copied_s = sem("strip_copied_s")
        tok_done = sem("tok_done")
        tok_biased = sem("tok_biased")
        tok_stored = [sem("tok_stored0"), sem("tok_stored1")]
        piece_in = [sem(f"piece_in{n}") for n in range(2)]
        piece_hi_set = sem("piece_hi_set")
        piece_lo = sem("piece_lo")
        w1_hi_set = sem("w1_hi_set")
        b1_t = sem("b1_t")
        b1_in = sem("b1_in")
        b1_copied = sem("b1_copied")
        consts_in = sem("consts_in")
        tokb_in = sem("tokb_in")
        wqk_in = sem("wqk_in")
        wqk_set = sem("wqk_set")
        strip_set = sem("strip_set")
        spare_out = sem("spare_out")

        ones_set = sem("ones_set")
        h_in = [sem("h_in0"), sem("h_in1")]
        hd_in = sem("hd_in")
        hd_biased = sem("hd_biased")
        ln1 = sem("ln1")
        rs1_set = sem("rs1_set")
        xn_set = sem("xn_set")
        xt_made = sem("xt_made")
        xt_copied = sem("xt_copied")
        qk_made = sem("qk_made")
        qk_copied = sem("qk_copied")
        qk_split = sem("qk_split")
        qk_out = [sem(f"qk_out{n}") for n in range(2)]
        stack_in = [[sem(f"stack_in{p}{n}") for n in range(2)] for p in range(2)]
        v_made = sem("v_made")
        v_copied = sem("v_copied")
        scores_made = sem("scores_made")
        max_taken = sem("max_taken")
        exp_done = sem("exp_done")
        sums_inverted = sem("sums_inverted")
        v_scaled = sem("v_scaled")
        pv_done = sem("pv_done")
        ctx_copied = sem("ctx_copied")
        proj_done = sem("proj_done")
        res_added = sem("res_added")
        h1_out = [sem("h1_out0"), sem("h1_out1")]
        ln2 = sem("ln2")
        rs2_set = sem("rs2_set")
        y_set = sem("y_set")
        y_split = sem("y_split")
        yt_made = sem("yt_made")
        yt_copied = sem("yt_copied")
        logits_made = sem("logits_made")
        route = sem("route")
        gap_exp = sem("gap_exp")
        weigh = sem("weigh")
        rank_made = sem("rank_made")
        place = sem("place")
        rows_out = [sem("rows_out0"), sem("rows_out1")]

        tab = sem("tab")
        pad_idx = sem("pad_idx")
        pads_out = sem("pads_out")
        tile_in = [sem(f"tile_in{n}") for n in range(4)]
        chain = sem("chain")
        rowt_zero = sem("rowt_zero")
        yt2_made = sem("yt2_made")
        yt2_copied = sem("yt2_copied")
        hid_made = sem("hid_made")
        gelu_done = sem("gelu_done")
        gelu_hi = sem("gelu_hi")
        gelu_lo = sem("gelu_lo")
        tile_done = sem("tile_done")
        b2_added = sem("b2_added")
        weighted = sem("weighted")
        added = [sem(f"added{n}") for n in range(4)]

        attn = ExitStack()
        with attn:
            wq_sb = sb(attn, "wq_sb", [DC + 1, 2, 2, DH, HALF])
            wk_sb = sb(attn, "wk_sb", [DC + 1, 2, 2, DH, HALF])
            wv_sb = sb(attn, "wv_sb", [DC + 1, 2, D])
            wo_sb = sb(attn, "wo_sb", [128, SC, D])
            router_t = sb(attn, "router_t", [DC, 2, E])
            before = sb(attn, "before", [SQ, SQ], BF16)
            ones_h = sb(attn, "ones_h", [SQ, 128], BF16)
            bo_rows = sb(attn, "bo_rows", [SQ, D])
            rev = sb(attn, "rev", [SQ, SC * E])
            rev_i = sb(attn, "rev_i", [SQ, SC * E], I32)
            token_no = sb(attn, "token_no", [SQ, SC * B], I32)
            half_neg = sb(attn, "half_neg", [SQ, SC])

            tok = ExitStack()
            with tok:
                image = [sb(tok, f"image{g}", [GR, C, P, GRID * P]) for g in range(NG)]
                strips = sb(tok, "strips", [128, 2, KTOK])
                strip = [strips[0:GR, n, :] for n in range(2)]
                tokw_nat = strips[0:DC, :, :]
                tokw = sb(tok, "tokw", [128, KC, D])
                tokb_rows = sb(tok, "tokb_rows", [GR, D])
                b1_nat = sb(tok, "b1_nat", [E * FC, 128])
                wq_nat = sb(tok, "wq_nat", [DC + 1, 2, H, DH])
                wk_nat = sb(tok, "wk_nat", [DC + 1, 2, H, DH])
                patches = [sb(tok, f"patches{n}", [128, KC, GR]) for n in range(2)]
                tokens = [sb(tok, f"tokens{n}", [GR, D]) for n in range(2)]
                piece = [sb(tok, f"piece{n}", [128, F]) for n in range(2)]
                piece_hi = sb(tok, "piece_hi", [128, F], BF16)

            q_stack = [sb(attn, f"q_stack{n}", [DC, H, S], BF16) for n in range(2)]
            k_stack = [sb(attn, f"k_stack{n}", [DC, H, S], BF16) for n in range(2)]
            probs = [sb(attn, f"probs{n}", [SQ, 4, SC, S]) for n in range(2)]
            h_a = [sb(attn, f"h_a{n}", [SQ, SC, D]) for n in range(2)]
            h_d = sb(attn, "h_d", [SQ, SC, D])
            stat1 = sb(attn, "stat1", [SQ, SC, 6])
            mv1 = sb(attn, "mv1", [SQ, SC, 2])
            ve1 = sb(attn, "ve1", [SQ, SC])
            nm1 = sb(attn, "nm1", [SQ, SC])
            rs1 = sb(attn, "rs1", [SQ, SC])
            xn = sb(attn, "xn", [SQ, SC, D])
            xt = sb(attn, "xt", [DC + 1, 2, S])
            qk_full = [sb(attn, f"qk_full{n}", [DC, S]) for n in range(2)]
            qk_bits = [sb(attn, f"qk_bits{n}", [DC, 3, S], BF16) for n in range(2)]
            v_raw = [sb(attn, f"v_raw{n}", [SQ, SC, H, DH]) for n in range(2)]
            v_over = [sb(attn, f"v_over{n}", [SQ, SC, 4, 2 * DH]) for n in range(2)]
            neg_max = sb(attn, "neg_max", [SQ, 3, SC, 4])
            sums = sb(attn, "sums", [SQ, 3, SC, 4])
            one_over = sb(attn, "one_over", [SQ, 3, SC, 4])
            ctx_t = sb(attn, "ctx_t", [128, SC, S])
            h1 = [sb(attn, f"h1_{n}", [SQ, SC, D]) for n in range(2)]
            stat2 = sb(attn, "stat2", [SQ, SC, 6])
            mv2 = sb(attn, "mv2", [SQ, SC, 2])
            ve2 = sb(attn, "ve2", [SQ, SC])
            nm2 = sb(attn, "nm2", [SQ, SC])
            rs2 = sb(attn, "rs2", [SQ, SC])
            y = sb(attn, "y", [SQ, SC, D])
            y_t = sb(attn, "y_t", [DC, 2, S])
            rows = [sb(attn, f"rows{n}", [SQ, SC, XROW], I32) for n in range(2)]
            logit = sb(attn, "logit", [SQ, SC, E])
            logit2 = sb(attn, "logit2", [SQ, SC, E])
            hit = sb(attn, "hit", [SQ, SC, E])
            first = sb(attn, "first", [SQ, SC, E])
            second = sb(attn, "second", [SQ, SC, E])
            either = sb(attn, "either", [SQ, SC, E], BF16)
            peak = sb(attn, "peak", [SQ, 4, SC])
            gap = sb(attn, "gap", [SQ, SC])
            gap_e = sb(attn, "gap_e", [SQ, SC])
            gap_1 = sb(attn, "gap_1", [SQ, SC])
            share = sb(attn, "share", [SQ, 2, SC])
            wone = sb(attn, "wone", [SQ, SC, E])
            wtwo = sb(attn, "wtwo", [SQ, SC, E])
            rank = sb(attn, "rank", [SQ, SC, E])
            at_one = sb(attn, "at_one", [SQ, SC, E])
            at_two = sb(attn, "at_two", [SQ, SC, E])
            where = [sb(attn, f"where{n}", [SQ, 2, SC], I32) for n in range(2)]

        moe = ExitStack()
        with moe:
            row_in = [sb(moe, f"row_in{n}", [128, XROW], I32) for n in range(4)]
            row_t = [sb(moe, f"row_t{n}", [128, 5, 128], BF16) for n in range(2)]
            gelu = [sb(moe, f"gelu{n}", [128, F]) for n in range(2)]
            g_hi = [sb(moe, f"g_hi{n}", [128, F], BF16) for n in range(2)]
            g_lo = [sb(moe, f"g_lo{n}", [128, F], BF16) for n in range(2)]
            with_b2 = sb(moe, "with_b2", [128, D])
            result = [sb(moe, f"result{n}", [128, D]) for n in range(4)]

        past, past_n = (p[0:1, 0:3, :, :].rearrange("o a c q -> o (a c q)")[:, 0:NTILE * E]
                        .rearrange("o (j e) -> o j e", e=E) for p in probs)

        SCORE, PV, MC, MA = bank[0:4], bank[4], bank[5], bank[6:8]
        patch_ps = [bank[0:2], bank[2:4]]
        tok_ps = bank[4:6]
        b1_ps = bank[6]
        rowt_ps = bank[0:2]
        hid_ps = [bank[2:4], bank[4:6]]
        tile_ps = bank[6:8]

        NSTEP = NG * GRID
        NPIECE = 5 * E

        def pieces_of(n):
            return [m for m in range(NPIECE) if m * NSTEP // NPIECE == n]

        def batches(eng, body):
            for i in range(-2, 2):
                body(Step(i // 2, i % 2, 2), lambda n, i=i: 0 <= i + n < B)
            last = B - 2
            with eng.Fori(1, last // 2) as turn:
                for k in range(2):
                    body(Step(turn, k, 2), lambda n: True)
            for i in range(last, B + 2):
                body(Step(i // 2, i % 2, 2), lambda n, i=i: 0 <= i + n < B)

        def expert_tiles(eng, body):
            for j in range(4):
                body(Step(0, j, 4), lambda n, j=j: 0 <= j + n < NTILE)
            with eng.Fori(1, NTILE // 4 - 1) as turn:
                for k in range(4):
                    body(Step(turn, k, 4), lambda n: True)
            for j in range(NTILE - 4, NTILE + 1):
                body(Step(j // 4, j % 4, 4), lambda n, j=j: 0 <= j + n < NTILE)

        block = top.enter_context(nc.Block())

        @block.sync
        def _(sp):
            sp.dma_start(tokw_nat[:, :, :], tok_w.rearrange("(c p) k -> p c k", p=DC)).then_inc(tokw_in, 16)
            for g in range(NG):
                for n in range(GB):
                    sp.dma_start(image[g][GRID * n:GRID * n + GRID, :, :, :].rearrange("r c y x -> r c (y x)"),
                                 x[g * GB + n, :, :, :].rearrange("c (g y) x -> g c (y x)", y=P)).then_inc(image_in[g], 16)

            column = patch_rows.rearrange("(r x) d -> r x d", x=GRID)
            for n in range(NSTEP):
                g, gx = n // GRID, n % GRID
                sp.wait_ge(tok_biased, n + 1)
                sp.dma_start(column[g * GR:(g + 1) * GR, gx, :], tokens[n % 2][:, :]).then_inc(tok_stored[n % 2], 16)
            for n in range(2):
                sp.wait_ge(tok_stored[n], 16 * (NSTEP // 2))

            def load_tokens(dst, b, done):
                pr = patch_rows.rearrange("(b n) d -> b n d", n=NPATCH)
                one = bass.ds(b.i, 1)
                rest = NPATCH - SQ
                sp.dma_start(dst[:, 0, :], pr[one, 0:SQ, :].rearrange("a n d -> (a n) d")).then_inc(done, 16)
                sp.dma_start(dst[0:rest, 1, :], pr[one, SQ:NPATCH, :].rearrange("a n d -> (a n) d")).then_inc(done, 16)
                sp.dma_start(dst[rest:SQ, 1, :], txt[one, 0:SQ - rest, :].rearrange("a n d -> (a n) d")).then_inc(done, 16)
                sp.dma_start(dst[:, 2, :], txt[one, SQ - rest:NTEXT, :].rearrange("a n d -> (a n) d")).then_inc(done, 16)

            def load_stack(b, half):
                o = b.odd
                hs = slice(HALF * half, HALF * half + HALF)
                for part, p0, copies in STACK_Q:
                    for n in range(copies):
                        src = qk_parts[o, half, part * DC:(part + 1) * DC, :].rearrange("(d h) q -> d (h q)", h=HALF)
                        sp.dma_start(q_stack[o][p0 + 16 * n:p0 + 16 * n + 16, hs, :].rearrange("p h q -> p (h q)"), src)\
                            .then_inc(stack_in[o][half], 16)
                for part, p0, parts in STACK_K:
                    src = qk_parts[o, 2 + half, part * DC:(part + parts) * DC, :].rearrange("(d h) q -> d (h q)", h=HALF)
                    sp.dma_start(k_stack[o][p0:p0 + 16 * parts, hs, :].rearrange("p h q -> p (h q)"), src)\
                        .then_inc(stack_in[o][half], 16)

            def store_parts(b, n):
                where_to = (0, 2, 1, 3)[n]
                sp.wait_ge(qk_split, 16 * b.i + 4 * n + 4)
                sp.dma_start(qk_parts[b.odd, where_to, :, :].rearrange("(c r) q -> r c q", c=3),
                             qk_bits[n % 2][:, :, :]).then_inc(qk_out[n // 2], 16)

            def iteration(i, has):
                a, c_, d_ = i + 1, i, i + -1
                if has(2):
                    up = i + 2
                    wait(sp, xn_set, SC * (up.i - 1))
                    load_tokens(h_a[up.odd], up, h_in[up.odd])
                if has(0):
                    wait(sp, res_added, SC * c_.i - SC)
                    settle(sp, sp_settled)
                if has(1):
                    store_parts(a, 0)
                    store_parts(a, 1)
                if has(-1):
                    sp.wait_ge(res_added, SC * d_.i + SC)
                    sp.dma_start(out[bass.ds(S * d_.i, S), :].rearrange("(c p) d -> p c d", p=SQ),
                                 h1[d_.odd][:, :, :]).then_inc(h1_out[d_.odd], 16)
                if has(0):
                    load_tokens(h_d, c_, hd_in)
                if has(1):
                    for half in range(2):
                        if half:
                            store_parts(a, 2)
                            store_parts(a, 3)
                        sp.wait_ge(qk_out[half], 32 * a.i + 32)
                        settle(sp, sp_settled)
                        wait(sp, scores_made, 36 * a.i - 54 + 18 * half)
                        load_stack(a, half)
            batches(sp, iteration)

            sp.wait_ge(tab, 1)
            sp.wait_ge(pads_out, 16 * E)
            sp.wait_ge(spare_out, 16 * (NSPARE + 1))
            for n in range(2):
                sp.wait_ge(rows_out[n], 96 * (B // 2))
                sp.wait_ge(h1_out[n], 16 * (B // 2))

            def tile(j, has):
                if has(0):
                    wait(sp, added[j.slot], 16 * j.turn)
                    row = sp.value_load(tile_row[0:1, bass.ds(j.i, 1)], min_val=0,
                                        max_val=E * REGION + (NSPARE - 1) * 128)
                    sp.dma_start(row_in[j.slot][:, :], expert_rows[bass.ds(row, 128), :]).then_inc(tile_in[j.slot], 16)

            expert_tiles(sp, tile)
            for n in range(4):
                sp.wait_ge(added[n], 16 * (NTILE // 4))

        @block.gpsimd
        def _(pool):
            g = nc.gpsimd
            g.memset(ident[:, :], 0.0).then_inc(made, 1)
            g.memset(before[:, :], 1.0).then_inc(made, 1)
            g.iota(lanes_i[:, :], [[1, 1]], base=0, channel_multiplier=1).then_inc(made, 1)
            g.iota(rev_i[:, :], [[0, SC], [-1, E]], base=E, channel_multiplier=0).then_inc(made, 1)
            g.iota(tile_no_i[:, :], [[1, NTILE]], base=0, channel_multiplier=0).then_inc(made, 1)
            g.iota(token_no[:, :], [[SQ, SC * B]], base=0, channel_multiplier=1).then_inc(made, 1)
            g.memset(pad_row[:, :], 0).then_inc(made, 1)
            g.memset(half_neg[:, :], -0.5).then_inc(made, 1)
            pool.wait_ge(made, 8)
            g.affine_select(out=ident[:, :], in_=ident[:, :], compare_op=ALU.not_equal, fill=1.0, base=0,
                            pattern=[[-1, 128]], channel_multiplier=1).then_inc(made, 1)
            g.affine_select(out=before[:, :], in_=before[:, :], compare_op=ALU.is_gt, fill=0.0, base=0,
                            pattern=[[1, SQ]], channel_multiplier=-1).then_inc(made, 1)
            g.iota(pad_row[:, TOKEN:TOKEN + 1], [[1, 1]], base=NTOK,
                   channel_multiplier=1).then_inc(made, 1)
            pool.wait_ge(made, 11)
            pool.wait_ge(made_v, 1)
            for n in range(NSPARE):
                pool.dma_start(expert_rows[E * REGION + 128 * n:E * REGION + 128 * n + 128, :], pad_row[:, :])\
                    .then_inc(spare_out, 16)
            pool.dma_start(out[NTOK:NTOK + 128, :], pad_row[:, 0:D].bitcast(F32)).then_inc(spare_out, 16)

            for n in range(NSTEP):
                gr, gx = n // GRID, n % GRID
                if gx == 0:
                    pool.wait_ge(image_in[gr], 16 * GB)
                wait(pool, strip_t, n - 1)
                if n == 0:
                    pool.wait_ge(tokw_t, 3)
                g.tensor_copy(strip[n % 2].rearrange("r (k x) -> r k x", x=P),
                              image[gr][:, :, :, P * gx:P * gx + P].rearrange("r c y x -> r (c y) x")).then_inc(strip_set, 1)

            pool.wait_ge(ones_set, 1)
            pool.wait_ge(consts_in, 16 * NCONST)

            def norm(b, src, stat_set, per, ve, nm, rs, rs_set, dst, dst_set, dst_free):
                pool.wait_ge(stat_set, per * b.i + per)
                g.tensor_tensor(rs[:, :], ve[:, :], half_neg[:, :], ALU.pow).then_inc(rs_set, 1)
                pool.wait_ge(rs_set, b.i + 1)
                for sem_, value in dst_free:
                    wait(pool, sem_, value)
                settle(pool, pool_settled)
                for c in range(SC):
                    g.tensor_scalar(dst[:, c, :], src[:, c, :], nm[:, c:c + 1], rs[:, c:c + 1],
                                    ALU.add, ALU.mult).then_inc(dst_set, 1)

            def scale_v(b, grp):
                pool.wait_ge(sums_inverted, 3 * b.i + grp + 1)
                if grp == 0:
                    pool.wait_ge(v_copied, 2 * b.i + 2)
                wait(pool, pv_done, 3 * b.i + grp - 1)
                g.tensor_tensor(v_over[(b.odd + grp) % 2][:, :, :, 0:DH].rearrange("p c j n -> p (c j) n"),
                                v_raw[b.odd][:, :, 4 * grp:4 * grp + 4, :],
                                one_over[:, grp, :, :].rearrange("p c (j o) -> p c j o", o=1)
                                .to_broadcast([SQ, SC, 4, DH]), ALU.mult).then_inc(v_scaled, 1)

            def split(b, n):
                o, done = n % 2, 16 * b.i + 4 * n
                pool.wait_ge(qk_copied, 4 * b.i + n + 1)
                if n < 2:
                    wait(pool, qk_out[1], 32 * b.i)
                else:
                    pool.wait_ge(qk_out[0], 32 * b.i + 32)
                settle(pool, pool_settled)
                g.tensor_copy(qk_bits[o][:, 0, :], qk_full[o][:, :]).then_inc(qk_split, 1)
                pool.wait_ge(qk_split, done + 1)
                g.tensor_tensor(qk_full[o][:, :], qk_full[o][:, :], qk_bits[o][:, 0, :], ALU.subtract).then_inc(qk_split, 1)
                pool.wait_ge(qk_split, done + 2)
                settle(pool, pool_settled)
                g.tensor_copy(qk_bits[o][:, 1, :], qk_full[o][:, :]).then_inc(qk_split, 1)
                pool.wait_ge(qk_split, done + 3)
                g.tensor_tensor(qk_bits[o][:, 2, :], qk_full[o][:, :], qk_bits[o][:, 1, :], ALU.subtract).then_inc(qk_split, 1)
                pool.wait_ge(qk_split, done + 4)

            def iteration(i, has):
                a, c_, d_, e_ = i + 1, i, i + -1, i + -2
                if has(-1):
                    pool.wait_ge(hd_in, 64 * d_.i + 64)
                    g.tensor_tensor(h_d[:, :, :], h_d[:, :, :], bo_rows[:, :].rearrange("p (o n) -> p o n", o=1)
                                    .to_broadcast([SQ, SC, D]), ALU.add).then_inc(hd_biased, 1)
                    scale_v(d_, 2)
                if has(1):
                    norm(a, h_a[a.odd], ln1, 8, ve1, nm1, rs1, rs1_set, xn, xn_set,
                         [(xt_made, 2 * a.i)])
                if has(-2):
                    pool.wait_ge(place, PLACE * e_.i + PLACE)
                    pool.wait_ge(weigh, 6 * e_.i + 6)
                    settle(pool, pool_settled)
                    for c in range(SC):
                        for slot in range(2):
                            g.indirect_dma_start(
                                out=expert_rows[:, :],
                                out_offset=bass.IndirectOffsetOnAxis(where[e_.odd][:, slot, c:c + 1], 0),
                                in_=rows[e_.odd][:, c, :], in_offset=None).then_inc(rows_out[e_.odd], 16)
                if has(0):
                    scale_v(c_, 0)
                if has(1):
                    split(a, 0)
                    split(a, 1)
                if has(-1):
                    norm(d_, h1[d_.odd], ln2, 8, ve2, nm2, rs2, rs2_set, y, y_set,
                         [(yt_made, 2 * d_.i)])
                if has(1):
                    split(a, 2)
                if has(0):
                    scale_v(c_, 1)
                if has(1):
                    split(a, 3)
                if has(-1):
                    pool.wait_ge(y_set, SC * d_.i + SC)
                    wait(pool, rows_out[d_.odd], 96 * d_.turn)
                    settle(pool, pool_settled)
                    r = rows[d_.odd][:, :, 0:YWORDS].bitcast(BF16)
                    g.tensor_copy(r[:, :, 0:D], y[:, :, :]).then_inc(y_split, 1)
                    g.tensor_copy(r[:, :, D:2 * D], y[:, :, :]).then_inc(y_split, 1)
                    g.tensor_copy(rows[d_.odd][:, :, TOKEN],
                                  token_no[:, bass.ds(SC * d_.i, SC)]).then_inc(y_split, 1)
                    pool.wait_ge(y_split, 4 * d_.i + 3)
                    g.tensor_tensor(r[:, :, 2 * D:3 * D], y[:, :, :], r[:, :, 0:D], ALU.subtract).then_inc(y_split, 1)
                    pool.wait_ge(y_split, 4 * d_.i + 4)

            batches(pool, iteration)

            pool.wait_ge(pad_idx, 1)
            for e in range(E):
                g.indirect_dma_start(out=expert_rows[:, :], out_offset=bass.IndirectOffsetOnAxis(pad_at[:, e:e + 1], 0),
                                     in_=pad_row[:, :], in_offset=None).then_inc(pads_out, 16)
            pool.wait_ge(tab, 1)
            pool.wait_ge(spare_out, 16 * (NSPARE + 1))
            for n in range(2):
                pool.wait_ge(h1_out[n], 16 * (B // 2))

            def tile(j, has):
                if has(-1):
                    t = j + -1
                    landed = [pool.value_load(tile_land[0:1, n, bass.ds(t.i, 1)], min_val=0, max_val=16 * NTILE)
                              for n in range(4)]
                    for n in range(4):
                        pool.wait_ge(added[n], landed[n])
                    pool.wait_ge(weighted, t.i + 1)
                    settle(pool, pool_settled)
                    g.indirect_dma_start(
                        out=out[:, :],
                        out_offset=bass.IndirectOffsetOnAxis(row_in[t.slot][:, TOKEN:TOKEN + 1], 0),
                        in_=result[t.slot][:, :], in_offset=None, compute_op=ALU.add).then_inc(added[t.slot], 16)

            expert_tiles(pool, tile)

        @block.scalar
        def _(act):
            s = nc.scalar
            act.dma_start(tokb_rows[:, :], tok_b.rearrange("(a n) -> a n", a=1).to_broadcast([GR, D])).then_inc(tokb_in, 16)
            act.dma_start(b1_nat[:, :], b1.rearrange("e (f p) -> (e f) p", p=128)).then_inc(b1_in, 16)
            for dst, w, bias in ((wq_nat, wq, bq), (wk_nat, wk, bk)):
                for c in range(2):
                    act.dma_start(dst[0:DC, c, :, :], w[:, DC * c:DC * c + DC, :].rearrange("h p n -> p h n")).then_inc(wqk_in, 16)
                act.dma_start(dst[DC:DC + 1, 1, :, :].rearrange("o h n -> o (h n)"),
                              bias.rearrange("(a h) n -> a (h n)", a=1)).then_inc(wqk_in, 16)
            for c in range(2):
                act.dma_start(wv_sb[0:DC, c, :].rearrange("p (h n) -> p h n", n=DH),
                              wv[:, DC * c:DC * c + DC, :].rearrange("h p n -> p h n")).then_inc(consts_in, 16)
            act.dma_start(wv_sb[DC:DC + 1, 1, :], bv.rearrange("(a h) n -> a (h n)", a=1)).then_inc(consts_in, 16)
            act.wait_ge(made_v, 2)
            for h in range(H):
                act.dma_start(wo_sb[32 * (h % 4):32 * (h % 4) + DH, h // 4, :], wo[DH * h:DH * h + DH, :]).then_inc(consts_in, 16)
            act.dma_start(bo_rows[:, :], bo.rearrange("(a n) -> a n", a=1).to_broadcast([SQ, D])).then_inc(consts_in, 16)
            with nc.allow_non_contiguous_dma(reason="1,536 weights of the router, transposed"):
                for c in range(2):
                    act.dma_start(router_t[:, c, :], router[:, DC * c:DC * c + DC].rearrange("e p -> p e")).then_inc(consts_in, 16)
            act.dma_start(b2_rows[:, :, :].rearrange("p e n -> p (e n)"),
                          b2.rearrange("(a e) n -> a (e n)", a=1).to_broadcast([128, E * D])).then_inc(consts_in, 16)

            def load_piece(n):
                e, k = divmod(n, 5)
                dst = piece[n % 2]
                wait(act, piece_lo, n - 1)
                wait(act, piece_hi_set, n - 1)
                done = piece_in[n % 2]
                if k == 0:
                    act.dma_start(dst[:, :], w1[e, 0:128, :]).then_inc(done, 32)
                elif k == 1:
                    act.dma_start(dst[0:64, :], w1[e, 128:D, :]).then_inc(done, 16)
                    act.dma_start(dst[64:128, :], w1[e, 0:64, :]).then_inc(done, 16)
                elif k == 2:
                    act.dma_start(dst[:, :], w1[e, 64:D, :]).then_inc(done, 32)
                else:
                    f = 3 * (k - 3)
                    act.dma_start(dst[:, 0:3 * D].rearrange("p (c n) -> p c n", c=3),
                                  w2[e, 128 * f:128 * f + 384, :].rearrange("(c p) n -> p c n", p=128)).then_inc(done, 32)

            def split_hi(n):
                e, k = divmod(n, 5)
                src = piece[n % 2]
                act.wait_ge(piece_in[n % 2], 32 * (n // 2) + 32)
                if k in (1, 2):
                    wait(act, piece_lo, n)
                    s.activation(piece_hi[:, :], src[:, :], ACT.Copy).then_inc(piece_hi_set, 1)
                    if k == 1:
                        s.activation(w1_parts[0:64, e, 1, :], src[0:64, :], ACT.Copy).then_inc(w1_hi_set, 1)
                elif k == 0:
                    s.activation(w1_parts[:, e, 0, :], src[:, :], ACT.Copy).then_inc(piece_hi_set, 1)
                else:
                    f = 3 * (k - 3)
                    s.activation(w2_hi[:, e, f:f + 3, :].rearrange("p c n -> p (c n)"), src[:, 0:3 * D], ACT.Copy)\
                        .then_inc(piece_hi_set, 1)

            act.wait_ge(b1_t, 1)
            s.activation(b1_cols[:, :], b1_ps[:, 0:E * FC], ACT.Copy).then_inc(b1_copied, 1)
            load_piece(0)
            load_piece(1)
            for n in range(NSTEP + 1):
                if n < NSTEP:
                    act.wait_ge(strip_t, n + 1)
                    if n >= 2:
                        act.wait_ge(tok_done, n - 1)
                    s.activation(patches[n % 2][:, 3:6, :].rearrange("p c r -> p (c r)"),
                                 patch_ps[n % 2][1][:, 0:3 * GR], ACT.Copy).then_inc(strip_copied_s, 1)
                for m in pieces_of(n):
                    split_hi(m)
                    if m + 2 < NPIECE:
                        load_piece(m + 2)

            act.wait_ge(ones_set, 1)

            def copy_ctx(b, grp):
                act.wait_ge(pv_done, 3 * b.i + grp + 1)
                if grp == 0:
                    wait(act, proj_done, SC * b.i)
                s.activation(ctx_t[:, grp, :], PV[:, 0:S], ACT.Copy).then_inc(ctx_copied, 1)

            def iteration(i, has):
                a, c_, d_, e_ = i + 1, i, i + -1, i + -2
                for h in range(H):
                    if has(0):
                        grp, j = h // 4, h % 4
                        if j == 0:
                            wait(act, pv_done, 3 * c_.i + grp - 1)
                        for c in range(SC):
                            act.wait_ge(max_taken, 36 * c_.i + 3 * h + c + 1)
                            s.activation(probs[(c_.odd + grp) % 2][:, j, c, :], SCORE[(3 * h + c) % 4][0:SQ, 0:S],
                                         ACT.Exp, bias=neg_max[:, grp, c, j:j + 1],
                                         accum_out=sums[:, grp, c, j:j + 1]).then_inc(exp_done, 1)
                    if h == 0 and has(-2):
                        act.wait_ge(route, ROUTE * e_.i + ROUTE)
                        s.activation(gap_e[:, :], gap[:, :], ACT.Exp).then_inc(gap_exp, 1)
                    if h == 3 and has(-1):
                        copy_ctx(d_, 2)
                    if h == 7 and has(0):
                        copy_ctx(c_, 0)
                    if h == 11 and has(0):
                        copy_ctx(c_, 1)
                    if h in (1, 2) and has(1):
                        n = h - 1
                        act.wait_ge(xt_made, 2 * a.i + n + 1)
                        wait(act, v_made, 2 * a.i)
                        s.activation(xt[0:DC, n, :], MA[n][0:DC, 0:S], ACT.Copy).then_inc(xt_copied, 1)
                    if h in (3, 4, 5, 6) and has(1):
                        n = h - 3
                        act.wait_ge(qk_made, 4 * a.i + n + 1)
                        wait(act, qk_split, 16 * a.i + 4 * n - 4)
                        s.activation(qk_full[n % 2][:, :], MA[n % 2][0:DC, 0:S], ACT.Copy).then_inc(qk_copied, 1)
                    if h in (7, 8) and has(1):
                        n = h - 7
                        nchunk = 2 - n
                        act.wait_ge(v_made, 2 * a.i + n + 1)
                        wait(act, v_scaled, 3 * a.i - 3)
                        s.activation(v_raw[a.odd][:, 2 * n:2 * n + nchunk, :, :].rearrange("p c h n -> p (c h n)"),
                                     MA[n][0:SQ, 0:nchunk * D], ACT.Copy).then_inc(v_copied, 1)
                    if h in (9, 10) and has(-1):
                        n = h - 9
                        act.wait_ge(yt_made, 2 * d_.i + n + 1)
                        wait(act, logits_made, d_.i)
                        s.activation(y_t[:, n, :], MC[0:DC, 0:S], ACT.Copy).then_inc(yt_copied, 1)

            batches(act, iteration)

            act.wait_ge(tab, 1)

            def tile(j, has):
                if has(1):
                    up = j + 1
                    act.wait_ge(yt2_made, up.i + 1)
                    wait(act, hid_made, 2 * (up.i - 1))
                    ps = rowt_ps[up.odd][:, :].bitcast(BF16)
                    s.activation(row_t[up.odd][:, 0:4, :].rearrange("p c n -> p (c n)"), ps[:, 0:512], ACT.Copy).then_inc(yt2_copied, 1)
                    s.activation(row_t[up.odd][0:64, 4, :], ps[0:64, 512:640], ACT.Copy).then_inc(yt2_copied, 1)
                if has(0):
                    e = act.value_load(tile_expert[0:1, bass.ds(j.i, 1)], min_val=0, max_val=E - 1)
                    for f in range(FC):
                        if f % 3 == 0:
                            act.wait_ge(hid_made, 2 * j.i + f // 3 + 1)
                            wait(act, gelu_lo, 2 * (j.i - 2) + f // 3 + 1)
                        last = s.activation(gelu[j.odd][:, 128 * f:128 * f + 128],
                                            hid_ps[j.odd][f // 3][:, 128 * (f % 3):128 * (f % 3) + 128],
                                            ACT.Gelu, bias=b1_cols[:, bass.ds(FC * e + f, 1)])
                        if f % 3 == 2:
                            last.then_inc(gelu_done, 1)

            act.wait_ge(yt2_made, 1)
            ps0 = rowt_ps[0][:, :].bitcast(BF16)
            s.activation(row_t[0][:, 0:4, :].rearrange("p c n -> p (c n)"), ps0[:, 0:512], ACT.Copy).then_inc(yt2_copied, 1)
            s.activation(row_t[0][0:64, 4, :], ps0[0:64, 512:640], ACT.Copy).then_inc(yt2_copied, 1)
            expert_tiles(act, tile)

        @block.vector
        def _(dve):
            v = nc.vector
            dve.wait_ge(made, 11)
            v.tensor_copy(ident_h[:, :], ident[:, :]).then_inc(made_v, 1)
            v.memset(wo_sb[:, :, :], 0.0).then_inc(made_v, 1)
            v.memset(ones_h[:, :], 1.0).then_inc(made_v, 1)
            v.tensor_copy(rev[:, :], rev_i[:, :]).then_inc(made_v, 1)
            v.tensor_copy(lanes[:, :], lanes_i[:, :]).then_inc(made_v, 1)
            for e in range(E):
                v.memset(carry[:, e:e + 1], float(e * REGION)).then_inc(made_v, 1)
            for n in range(3):
                dve.wait_ge(tokw_t, n + 1)
                v.tensor_copy(tokw[:, 2 * n:2 * n + 2, :].rearrange("p c n -> p (c n)"),
                              bank[n][:, 0:2 * D]).then_inc(tokw_copied, 1)

            def split_lo(n):
                e, k = divmod(n, 5)
                src = piece[n % 2]
                dve.wait_ge(piece_hi_set, n + 1)
                if k == 0:
                    v.sem_inc(piece_lo, 1)
                elif k == 1:
                    dve.wait_ge(w1_hi_set, e + 1)
                    v.tensor_tensor(w1_parts[64:128, e, 1, :], src[64:128, :], piece_hi[64:128, :], ALU.subtract).then_inc(piece_lo, 1)
                elif k == 2:
                    v.tensor_tensor(w1_parts[:, e, 2, :], src[:, :], piece_hi[:, :], ALU.subtract).then_inc(piece_lo, 1)
                else:
                    f = 3 * (k - 3)
                    v.tensor_tensor(w2_lo[:, e, f:f + 3, :].rearrange("p c n -> p (c n)"), src[:, 0:3 * D],
                                    w2_hi[:, e, f:f + 3, :].rearrange("p c n -> p (c n)"), ALU.subtract).then_inc(piece_lo, 1)

            dve.wait_ge(wqk_in, 16 * 6)
            for src, dst in ((wq_nat, wq_sb), (wk_nat, wk_sb)):
                for c, rows_ in ((0, DC), (1, DC + 1)):
                    for half in range(2):
                        v.tensor_scalar(dst[0:rows_, c, half, :, :],
                                        src[0:rows_, c, HALF * half:HALF * half + HALF, :].rearrange("p h n -> p n h"),
                                        float(DH) ** -0.5 if dst is wq_sb else 1.0, None, ALU.mult).then_inc(wqk_set, 1)
            dve.wait_ge(tokb_in, 16)
            for n in range(NSTEP + 1):
                if n < NSTEP:
                    dve.wait_ge(strip_t, n + 1)
                    if n >= 2:
                        dve.wait_ge(tok_done, n - 1)
                    v.tensor_copy(patches[n % 2][:, 0:3, :].rearrange("p c r -> p (c r)"),
                                  patch_ps[n % 2][0][:, 0:3 * GR]).then_inc(strip_copied_v, 1)
                if n >= 1:
                    dve.wait_ge(tok_done, n)
                    wait(dve, tok_stored[(n - 1) % 2], 16 * ((n - 1) // 2))
                    v.tensor_tensor(tokens[(n - 1) % 2][:, :], tok_ps[(n - 1) % 2][0:GR, 0:D], tokb_rows[:, :], ALU.add).then_inc(tok_biased, 1)
                for m in pieces_of(n):
                    split_lo(m)

            dve.wait_ge(tok_done, NSTEP)
            for n in range(2):
                dve.wait_ge(tok_stored[n], 16 * (NSTEP // 2))
            for n in range(2):
                v.memset(v_over[n][:, :, :, DH:2 * DH], 0.0)
            v.memset(xt[DC:DC + 1, :, :], 1.0).then_inc(ones_set, 1)

            def statistics(b, src, parts, stat, mv, ve, nm, done):
                base_ = 8 * b.i
                if parts:
                    for c in range(SC):
                        v.bn_stats(stat[:, c, :], src[:, c, :]).then_inc(done, 1)
                dve.wait_ge(done, base_ + 3)
                settle(dve, dve_settled)
                for c in range(SC):
                    v.bn_aggr(mv[:, c, :], stat[:, c, :]).then_inc(done, 1)
                dve.wait_ge(done, base_ + 6)
                v.tensor_scalar(ve[:, :], mv[:, :, 1], EPS, None, ALU.add).then_inc(done, 1)
                v.tensor_scalar(nm[:, :], mv[:, :, 0], -1.0, None, ALU.mult).then_inc(done, 1)

            def invert(b, grp):
                dve.wait_ge(exp_done, 36 * b.i + 12 * grp + 12)
                v.reciprocal(one_over[:, grp, :, :].rearrange("p c j -> p (c j)"),
                             sums[:, grp, :, :].rearrange("p c j -> p (c j)")).then_inc(sums_inverted, 1)

            def bc(t):
                return t.rearrange("p (c o) -> p c o", o=1).to_broadcast([SQ, SC, E])

            def flat(t):
                return t[:, :, :].rearrange("p c e -> p (c e)")

            def choose(b):
                k = [0]

                def link(ins):
                    k[0] += 1
                    ins.then_inc(route, 1)
                    dve.wait_ge(route, ROUTE * b.i + k[0])

                dve.wait_ge(logits_made, b.i + 1)
                wait(dve, weigh, 6 * b.i)
                link(v.tensor_copy(flat(logit), MC[0:SQ, 0:SC * E]))
                for src, hot, n in ((logit, first, 0), (logit2, second, 1)):
                    link(v.tensor_reduce(peak[:, 2 * n, :], src[:, :, :], AX.X, ALU.max))
                    link(v.tensor_tensor(hit[:, :, :], src[:, :, :], bc(peak[:, 2 * n, :]), ALU.is_ge))
                    link(v.tensor_tensor(flat(hit), flat(hit), rev[:, :], ALU.mult))
                    link(v.tensor_reduce(peak[:, 2 * n + 1, :], hit[:, :, :], AX.X, ALU.max))
                    link(v.tensor_tensor(hot[:, :, :], hit[:, :, :], bc(peak[:, 2 * n + 1, :]), ALU.is_equal))
                    if n == 0:
                        link(v.scalar_tensor_tensor(flat(logit2), flat(first), -3e38, flat(logit), ALU.mult, ALU.add))
                link(v.tensor_tensor(either[:, :, :], first[:, :, :], second[:, :, :], ALU.add))
                link(v.tensor_tensor(gap[:, :], peak[:, 2, :], peak[:, 0, :], ALU.subtract))
                assert k[0] == ROUTE

            def weights(b):
                k = [0]

                def link(ins):
                    k[0] += 1
                    ins.then_inc(weigh, 1)
                    dve.wait_ge(weigh, 6 * b.i + k[0])

                dve.wait_ge(gap_exp, b.i + 1)
                link(v.tensor_scalar(gap_1[:, :], gap_e[:, :], 1.0, None, ALU.add))
                link(v.reciprocal(share[:, 0, :], gap_1[:, :]))
                link(v.tensor_tensor(share[:, 1, :], gap_e[:, :], share[:, 0, :], ALU.mult))
                link(v.tensor_tensor(wone[:, :, :], first[:, :, :], bc(share[:, 0, :]), ALU.mult))
                link(v.tensor_tensor(wtwo[:, :, :], second[:, :, :], bc(share[:, 1, :]), ALU.mult))
                dve.wait_ge(y_split, 4 * b.i + 4)
                link(v.tensor_tensor(rows[b.odd][:, :, YWORDS:TOKEN].bitcast(F32), wone[:, :, :], wtwo[:, :, :], ALU.add))

            def places(b):
                k = [0]

                def link(ins):
                    k[0] += 1
                    ins.then_inc(place, 1)
                    dve.wait_ge(place, PLACE * b.i + k[0])

                dve.wait_ge(rank_made, b.i + 1)
                link(v.tensor_tensor(rank[:, :, :], MC[0:SQ, 0:SC * E].rearrange("p (c e) -> p c e", c=SC),
                                     carry[0:SQ, :].rearrange("p (o e) -> p o e", o=1).to_broadcast([SQ, SC, E]), ALU.add))
                link(v.tensor_tensor(carry[:, :], MC[:, SC * E:SC * E + E], carry[:, :], ALU.add))
                v.tensor_tensor(at_one[:, :, :], first[:, :, :], rank[:, :, :], ALU.mult)
                link(v.tensor_tensor(at_two[:, :, :], second[:, :, :], rank[:, :, :], ALU.mult))
                wait(dve, rows_out[b.odd], 96 * b.turn)
                with nc.allow_low_precision(reason="one of the 8 summands is a row number, the others are 0"):
                    v.tensor_reduce(where[b.odd][:, 0, :], at_one[:, :, :], AX.X, ALU.add)
                    link(v.tensor_reduce(where[b.odd][:, 1, :], at_two[:, :, :], AX.X, ALU.add))

            def iteration(i, has):
                a, c_, d_, e_ = i + 1, i, i + -1, i + -2
                for h in range(H):
                    if has(0):
                        for c in range(SC):
                            dve.wait_ge(scores_made, 36 * c_.i + 3 * h + c + 1)
                            v.tensor_reduce(neg_max[:, h // 4, c, h % 4:h % 4 + 1], SCORE[(3 * h + c) % 4][0:SQ, 0:S],
                                            AX.X, ALU.max, negate=True).then_inc(max_taken, 1)
                    if h == 0 and has(-1):
                        invert(d_, 2)
                    if h == 0 and has(1):
                        dve.wait_ge(h_in[a.odd], 64 * a.turn + 64)
                        wait(dve, rs1_set, a.i)
                        wait(dve, xn_set, SC * a.i)
                        statistics(a, h_a[a.odd], True, stat1, mv1, ve1, nm1, ln1)
                    if h == 0 and has(-2):
                        weights(e_)
                    if h == 1 and has(-2):
                        places(e_)
                    if h == 4 and has(0):
                        invert(c_, 0)
                    if h == 8 and has(0):
                        invert(c_, 1)
                    if h in (4, 5, 6) and has(-1):
                        c = h - 4
                        dve.wait_ge(proj_done, SC * d_.i + c + 1)
                        if c == 0:
                            dve.wait_ge(hd_biased, d_.i + 1)
                            wait(dve, h1_out[d_.odd], 16 * d_.turn)
                            wait(dve, y_set, SC * (d_.i - 1))
                        v.tensor_tensor(h1[d_.odd][:, c, :], MC[0:SQ, 0:D], h_d[:, c, :], ALU.add).then_inc(res_added, 1)
                        dve.wait_ge(res_added, SC * d_.i + c + 1)
                        v.bn_stats(stat2[:, c, :], h1[d_.odd][:, c, :]).then_inc(ln2, 1)
                        if c == 2:
                            wait(dve, rs2_set, d_.i)
                            wait(dve, y_set, SC * d_.i)
                            statistics(d_, None, False, stat2, mv2, ve2, nm2, ln2)
                    if h == 11 and has(-1):
                        choose(d_)

            batches(dve, iteration)

            k = [0]

            def link(ins):
                k[0] += 1
                ins.then_inc(chain, 1)
                dve.wait_ge(chain, k[0])

            v.tensor_scalar(pad_at[:, :], carry[:, :], lanes[:, 0:1], None, ALU.add).then_inc(pad_idx, 1)
            for e in range(E):
                link(v.tensor_scalar(count[:, e:e + 1], carry[0:1, e:e + 1], 127.0 - e * REGION, None, ALU.add))
            link(v.tensor_copy(count_i[:, :], count[:, :]))
            link(v.tensor_scalar(count_i[:, :], count_i[:, :], 7, None, ALU.arith_shift_right))
            link(v.tensor_copy(tiles[:, :], count_i[:, :]))
            link(v.tensor_copy(ends[:, 0:1], tiles[:, 0:1]))
            for e in range(1, E):
                link(v.tensor_tensor(ends[:, e:e + 1], ends[:, e - 1:e], tiles[:, e:e + 1], ALU.add))
            link(v.tensor_copy(tile_no[:, :], tile_no_i[:, :]))
            wide = [1, NTILE, E]
            link(v.tensor_tensor(past[:, :, :], tile_no[:, :].rearrange("p (j o) -> p j o", o=1).to_broadcast(wide),
                                 ends[:, :].rearrange("p (o e) -> p o e", o=1).to_broadcast(wide), ALU.is_ge))
            link(v.tensor_reduce(owner[:, :], past[:, :, :], AX.X, ALU.add))
            link(v.tensor_tensor(past_n[:, :, :], past[:, :, :], tiles[:, :].rearrange("p (o e) -> p o e", o=1).to_broadcast(wide), ALU.mult))
            link(v.tensor_reduce(begun[:, :], past_n[:, :, :], AX.X, ALU.add))
            link(v.tensor_tensor(step_no[:, :], tile_no[:, :], begun[:, :], ALU.subtract))
            link(v.tensor_scalar(base[:, :], owner[:, :], float(REGION), None, ALU.mult))
            link(v.scalar_tensor_tensor(tile_row[:, :], step_no[:, :], 128.0, base[:, :], ALU.mult, ALU.add))
            link(v.tensor_scalar(tile_expert[:, :], owner[:, :], float(E - 1), None, ALU.min))
            link(v.tensor_tensor(spare[:, :], step_no[:, :], past[:, :, E - 1], ALU.mult))
            link(v.tensor_tensor(spare[:, :], spare[:, :], begun[:, :], ALU.add))
            for n in range(4):
                link(v.tensor_scalar(land[:, :], spare[:, :], float(3 - n), None, ALU.add))
                link(v.tensor_scalar(tile_land[:, n, :], land[:, :], 2, 4, ALU.arith_shift_right, ALU.arith_shift_left))
            v.tensor_copy(count[:, :], tiles[:, :]).then_inc(tab, 1)
            for n in range(2):
                dve.wait_ge(rows_out[n], 96 * (B // 2))
                dve.wait_ge(h1_out[n], 16 * (B // 2))
            for n in range(2):
                v.memset(row_t[n][64:128, 4, :], 0.0).then_inc(rowt_zero, 1)

            def tile(j, has):
                if has(0):
                    for half in range(2):
                        sl = slice(F // 2 * half, F // 2 * half + F // 2)
                        dve.wait_ge(gelu_done, 2 * j.i + half + 1)
                        wait(dve, tile_done, j.i - 1)
                        v.tensor_copy(g_hi[j.odd][:, sl], gelu[j.odd][:, sl]).then_inc(gelu_hi, 1)
                        dve.wait_ge(gelu_hi, 2 * j.i + half + 1)
                        v.tensor_tensor(g_lo[j.odd][:, sl], gelu[j.odd][:, sl], g_hi[j.odd][:, sl], ALU.subtract).then_inc(gelu_lo, 1)
                if has(-1):
                    t = j + -1
                    dve.wait_ge(tile_done, t.i + 1)
                    wait(dve, weighted, t.i)
                    e = dve.value_load(tile_expert[0:1, bass.ds(t.i, 1)], min_val=0, max_val=E - 1)
                    v.tensor_tensor(with_b2[:, :], tile_ps[t.odd][:, 0:D],
                                    b2_rows[:, bass.ds(e, 1), :].rearrange("p a n -> p (a n)"), ALU.add).then_inc(b2_added, 1)
                    dve.wait_ge(b2_added, t.i + 1)
                    wait(dve, added[t.slot], 16 * t.turn)
                    v.tensor_scalar(result[t.slot][:, :], with_b2[:, :],
                                    row_in[t.slot][:, YWORDS:TOKEN].bitcast(F32)[:, bass.ds(e, 1)], None,
                                    ALU.mult).then_inc(weighted, 1)

            expert_tiles(dve, tile)

        @block.tensor
        def _(pe):
            mm, turn_ = nc.tensor.matmul, nc.tensor.transpose

            def product(dst, pairs):
                for n, (lhs, rhs) in enumerate(pairs):
                    last = mm(dst, lhs, rhs, start=(n == 0), stop=(n == len(pairs) - 1))
                return last

            pe.wait_ge(made, 11)
            pe.wait_ge(tokw_in, 16)
            for n in range(3):
                for k in (2 * n, 2 * n + 1):
                    for c in range(2):
                        last = turn_(bank[n][:, D * (k % 2) + DC * c:D * (k % 2) + DC * c + DC],
                                     tokw_nat[:, c, 128 * k:128 * k + 128], ident[0:DC, 0:DC])
                last.then_inc(tokw_t, 1)
            pe.wait_ge(b1_in, 16)
            turn_(b1_ps[:, 0:E * FC], b1_nat[:, :], ident[0:E * FC, 0:E * FC]).then_inc(b1_t, 1)
            pe.wait_ge(tokw_copied, 3)
            for n in range(NSTEP + 1):
                if n < NSTEP:
                    pe.wait_ge(strip_set, n + 1)
                    if n >= 2:
                        pe.wait_ge(strip_copied_v, n - 1)
                        pe.wait_ge(strip_copied_s, n - 1)
                    for k in range(KC):
                        last = turn_(patch_ps[n % 2][k // 3][:, GR * (k % 3):GR * (k % 3) + GR],
                                     strip[n % 2][:, 128 * k:128 * k + 128],
                                     ident[0:GR, 0:GR])
                    last.then_inc(strip_t, 1)
                if n >= 1:
                    m = n - 1
                    pe.wait_ge(strip_copied_v, m + 1)
                    pe.wait_ge(strip_copied_s, m + 1)
                    wait(pe, tok_biased, m - 1)
                    product(tok_ps[m % 2][0:GR, 0:D],
                            [(patches[m % 2][:, k, :], tokw[:, k, :]) for k in range(KC)]).then_inc(tok_done, 1)

            pe.wait_ge(ones_set, 1)
            pe.wait_ge(made_v, 5 + E)
            pe.wait_ge(consts_in, 16 * NCONST)
            pe.wait_ge(wqk_set, 8)
            pe.wait_ge(b1_copied, 1)

            def probs_values(b, grp, c):
                if c == 0:
                    pe.wait_ge(v_scaled, 3 * b.i + grp + 1)
                    wait(pe, ctx_copied, 3 * b.i + grp)
                for j in range(4):
                    last = mm(PV[32 * j:32 * j + 32, 0:S], v_over[(b.odd + grp) % 2][:, c, j, :],
                              probs[(b.odd + grp) % 2][:, j, c, :], start=(c == 0), stop=(c == SC - 1))
                if c == SC - 1:
                    last.then_inc(pv_done, 1)

            def iteration(i, has):
                a, c_, d_, e_ = i + 1, i, i + -1, i + -2
                for h in range(H):
                    half = h // HALF
                    for c in range(SC):
                        if not has(0):
                            break
                        if h % HALF == 0 and c == 0:
                            pe.wait_ge(stack_in[c_.odd][half], 144 * c_.turn + 144)
                        wait(pe, exp_done, 36 * c_.i + 3 * h + c - 3)
                        mm(SCORE[(3 * h + c) % 4][0:SQ, 0:S], k_stack[c_.odd][:, h, SQ * c:SQ * c + SQ],
                           q_stack[c_.odd][:, h, :], start=True, stop=True).then_inc(scores_made, 1)
                    if 1 <= h < 4 and has(-1):
                        probs_values(d_, 2, h - 1)
                    if 5 <= h < 8 and has(0):
                        probs_values(c_, 0, h - 5)
                    if 9 <= h < 12 and has(0):
                        probs_values(c_, 1, h - 9)
                    if h == 1 and has(-2):
                        pe.wait_ge(route, ROUTE * e_.i + ROUTE)
                        for c in range(SC):
                            product(MC[0:SQ, E * c:E * c + E],
                                    [(ones_h[:, 0:SQ], either[:, n, :]) for n in range(c)] +
                                    [(before[:, :], either[:, c, :])])
                        product(MC[:, SC * E:SC * E + E],
                                [(ones_h[:, :], either[:, n, :]) for n in range(SC)]).then_inc(rank_made, 1)
                    if h in (4, 5, 6) and has(-1):
                        c = h - 4
                        pe.wait_ge(ctx_copied, 3 * d_.i + 3)
                        if c:
                            pe.wait_ge(res_added, 3 * d_.i + c)
                        elif has(-2):
                            pe.wait_ge(place, PLACE * e_.i + 2)
                        product(MC[0:SQ, 0:D], [(ctx_t[:, n, SQ * c:SQ * c + SQ], wo_sb[:, n, :]) for n in range(SC)])\
                            .then_inc(proj_done, 1)
                    if h in (9, 10) and has(-1):
                        n = h - 9
                        pe.wait_ge(y_set, SC * d_.i + SC)
                        if n == 0:
                            pe.wait_ge(res_added, 3 * d_.i + 3)
                        else:
                            pe.wait_ge(yt_copied, 2 * d_.i + 1)
                        for c in range(SC):
                            last = turn_(MC[0:DC, SQ * c:SQ * c + SQ], y[:, c, DC * n:DC * n + DC], ident[0:SQ, 0:SQ])
                        last.then_inc(yt_made, 1)
                    if h == 11 and has(-1):
                        pe.wait_ge(yt_copied, 2 * d_.i + 2)
                        for c in range(SC):
                            last = product(MC[0:SQ, E * c:E * c + E],
                                           [(y_t[:, n, SQ * c:SQ * c + SQ], router_t[:, n, :]) for n in range(2)])
                        last.then_inc(logits_made, 1)
                    if h in (1, 2) and has(1):
                        n = h - 1
                        pe.wait_ge(xn_set, SC * a.i + SC)
                        if has(0):
                            pe.wait_ge(v_copied, 2 * c_.i + n + 1)
                        for c in range(SC):
                            last = turn_(MA[n][0:DC, SQ * c:SQ * c + SQ], xn[:, c, DC * n:DC * n + DC], ident[0:SQ, 0:SQ])
                        last.then_inc(xt_made, 1)
                    if h in (3, 4, 5, 6) and has(1):
                        n = h - 3
                        pe.wait_ge(xt_copied, 2 * a.i + 2)
                        if n >= 2:
                            pe.wait_ge(qk_copied, 4 * a.i + n - 1)
                        w = (wq_sb, wk_sb)[n % 2]
                        product(MA[n % 2][0:DC, 0:S],
                                [(w[0:DC, 0, n // 2, :, :].rearrange("p n h -> p (n h)"), xt[0:DC, 0, :]),
                                 (w[:, 1, n // 2, :, :].rearrange("p n h -> p (n h)"), xt[:, 1, :])]).then_inc(qk_made, 1)
                    if h in (7, 8) and has(1):
                        n = h - 7
                        pe.wait_ge(qk_copied, 4 * a.i + n + 3)
                        for c in ((0, 1), (2,))[n]:
                            last = product(MA[n][0:SQ, D * (c % 2):D * (c % 2) + D],
                                           [(xt[0:DC, 0, SQ * c:SQ * c + SQ], wv_sb[0:DC, 0, :]),
                                            (xt[:, 1, SQ * c:SQ * c + SQ], wv_sb[:, 1, :])])
                        last.then_inc(v_made, 1)

            batches(pe, iteration)

            pe.wait_ge(tab, 1)
            pe.wait_ge(rowt_zero, 2)

            def rows_t(j):
                pe.wait_ge(tile_in[j.slot], 16 * j.turn + 16)
                wait(pe, yt2_copied, 2 * j.i - 2)
                ps = rowt_ps[j.odd][:, :].bitcast(BF16)
                for k in range(5):
                    n = min(128, 3 * D - 128 * k)
                    last = turn_(ps[0:n, 128 * k:128 * k + 128], row_in[j.slot][:, 0:YWORDS].bitcast(BF16)[:, 128 * k:128 * k + n], ident_h[:, :])
                last.then_inc(yt2_made, 1)

            def tile(j, has):
                if has(0):
                    pe.wait_ge(yt2_copied, 2 * j.i + 2)
                    wait(pe, gelu_done, 2 * j.i - 2)
                    settle(pe, pe_settled)
                    e = pe.value_load(tile_expert[0:1, bass.ds(j.i, 1)], min_val=0, max_val=E - 1)
                    for f in range(FC):
                        last = product(hid_ps[j.odd][f // 3][:, 128 * (f % 3):128 * (f % 3) + 128],
                                       [(w1_parts[:, bass.ds(e, 1), W1CHUNK[k], 128 * f:128 * f + 128]
                                         .rearrange("p a n -> p (a n)"), row_t[j.odd][:, k, :]) for k in range(5)])
                        if f % 3 == 2:
                            last.then_inc(hid_made, 1)
                if has(1):
                    rows_t(j + 1)
                if has(-1):
                    d_ = j + -1
                    pe.wait_ge(gelu_lo, 2 * d_.i + 2)
                    wait(pe, b2_added, d_.i - 1)
                    settle(pe, pe_settled)
                    e = pe.value_load(tile_expert[0:1, bass.ds(d_.i, 1)], min_val=0, max_val=E - 1)
                    pairs = []
                    for f in range(FC):
                        hi, lo = (g[d_.odd][:, 128 * f:128 * f + 128] for g in (g_hi, g_lo))
                        whi, wlo = (w[:, bass.ds(e, 1), f, :].rearrange("p a n -> p (a n)") for w in (w2_hi, w2_lo))
                        pairs += [(hi, whi), (hi, wlo), (lo, whi)]
                    product(tile_ps[d_.odd][:, 0:D], pairs).then_inc(tile_done, 1)

            rows_t(Step(0, 0, 4))
            expert_tiles(pe, tile)


_INS = ["x", "txt", "L0_tok_W", "L0_tok_b", "L0_attn_Wq", "L0_attn_bq", "L0_attn_Wk", "L0_attn_bk", "L0_attn_Wv",
        "L0_attn_bv", "L0_attn_Wo", "L0_attn_bo", "L0_ffn_router_w", "L0_ffn_w1", "L0_ffn_b1", "L0_ffn_w2", "L0_ffn_b2"]


def kernel(**inputs):
    import numpy as _np
    import concourse.bacc as _bacc
    from concourse import mybir as _mybir
    from concourse.bass_utils import run_bass_kernel_spmd as _run

    nc = _bacc.Bacc("TRN2", target_bir_lowering=False, num_devices=1)
    arrays, args = {}, []
    for name in _INS:
        a = _np.ascontiguousarray(inputs[name])
        if name == "L0_tok_W":
            a = a.reshape(a.shape[0], -1)
        arrays[f"in_{name}"] = a
        args.append(nc.dram_tensor(f"in_{name}", a.shape, _mybir.dt.from_np(a.dtype), kind="ExternalInput").ap())
    batches = inputs["x"].shape[0]
    out = nc.dram_tensor("out_rows", (batches * S + 128, D), _mybir.dt.float32, kind="ExternalOutput").ap()
    fusion_layer(nc, *args, out)
    r = _run(nc, [arrays], core_ids=[0])
    return r.results[0]["out_rows"][:batches * S].reshape(batches, S, D)
```

```python
import concourse.bass as bass
from concourse import mybir
from contextlib import ExitStack

F32 = mybir.dt.float32
BF16 = mybir.dt.bfloat16
I32 = mybir.dt.int32
ALU = mybir.AluOpType
ACT = mybir.ActivationFunctionType
AX = mybir.AxisListType

E, TOPK = 8, 2
H, DH = 12, 16
D = H * DH
DC = D // 2
F = 768
FC = F // 128
C, P, GRID = 3, 16, 14
KTOK = C * P * P
KC = KTOK // 128
NPATCH, NTEXT = GRID * GRID, 128
S = NPATCH + NTEXT
SC, SQ = 3, 108
HALF = H // 2
EPS = 1e-5
RING = 8
TILE = 256
YWORDS = 2 * D // 2
TOKEN = YWORDS + E
XROW = TOKEN + 1
STACK_Q = ((0, 0, 3), (1, 48, 2), (2, 80, 1))
STACK_K = ((0, 0, 3), (0, 48, 2), (0, 80, 1))
QK_TILES = (((0, 0, 0, 96), (1, 0, 96, 32)), ((1, 32, 0, 64), (2, 0, 64, 64)), ((2, 64, 0, 32), (3, 0, 32, 96)))
XK = (128, D - 128 + 1)
ONES = D - 128
ROUTE = 14
PLACE = 4
HI_A, LO_A, HI_B, LO_B = range(4)
W1_TIMES_Y = ((HI_A, 0), (LO_A, 0), (HI_B, 1), (LO_B, 1), (HI_A, 2))
WO_AT = [(0, 32 * (h % 4) + DH * (h // 4)) if h < 8 else (1, 32 * (h % 4)) for h in range(H)]
BO_ROW = DH


class Step:

    def __init__(self, turn, k, of):
        self.of, self.turn, self.slot = of, turn + k // of, k % of
        self.odd = self.slot % 2
        self.i = of * self.turn + self.slot

    def __add__(self, n):
        return Step(self.turn, self.slot + n, self.of)

    def fours(self):
        return self.of // 4 * self.turn + self.slot // 4


def wait(eng, sem, value):
    if not (isinstance(value, int) and value <= 0):
        eng.wait_ge(sem, value)


def settle(eng, settled):
    eng.sem_inc(settled, 1)


def fusion_layer(nc, x, txt, tok_w, tok_b, wq, bq, wk, bk, wv, bv, wo, bo, router, w1, b1, w2, b2, out):
    B = x.shape[0]
    NTOK = B * S
    REGION = NTOK + TILE
    NTILE = (TOPK * NTOK + E * (TILE - 1)) // TILE
    NSPARE = E
    GB = 8
    NG = B // GB
    NCONST = H + 1 + 3 + 2
    GR = GB * GRID

    patch_rows = nc.dram_tensor("patch_rows", [B * NPATCH, D], F32, kind="Internal").ap()
    qk_parts = nc.dram_tensor("qk_parts", [2, 4, 3 * DC, S], BF16, kind="Internal").ap()
    expert_rows = nc.dram_tensor("expert_rows", [E * REGION + NSPARE * TILE, XROW], I32, kind="Internal").ap()

    top = ExitStack()
    with top:
        def sem(name):
            return top.enter_context(nc.semaphore(name))

        def sb(stack, name, shape, dt=F32):
            return stack.enter_context(nc.sbuf_tensor(name, shape, dt))

        bank = [top.enter_context(nc.psum_tensor(f"bank{n}", [128, 512], F32)) for n in range(8)]

        w1_parts = sb(top, "w1_parts", [128, E, 4, F], BF16)
        w2_hi = sb(top, "w2_hi", [128, E, FC, D], BF16)
        w2_lo = sb(top, "w2_lo", [128, E, FC, D], BF16)
        b1_cols = sb(top, "b1_cols", [128, E * FC])
        ident = sb(top, "ident", [128, 128])
        ident_h = sb(top, "ident_h", [128, 128], BF16)
        pad_rows = sb(top, "pad_rows", [128, 2, XROW], I32)
        carry = sb(top, "carry", [128, E])
        tile_row = sb(top, "tile_row", [1, NTILE], I32)
        tile_expert = sb(top, "tile_expert", [1, NTILE + 4], I32)
        tile_land = sb(top, "tile_land", [1, 4, NTILE], I32)
        land = sb(top, "land", [1, NTILE], I32)

        gelu_table = sb(top, "gelu_table", [128, 1])

        count = sb(top, "count", [1, E])
        region = sb(top, "region", [1, E])
        count_i = sb(top, "count_i", [1, E], I32)
        tiles = sb(top, "tiles", [1, E])
        ends = sb(top, "ends", [1, E])
        tile_no = sb(top, "tile_no", [1, NTILE])
        tile_no_i = sb(top, "tile_no_i", [1, NTILE], I32)
        owner = sb(top, "owner", [1, NTILE])
        begun = sb(top, "begun", [1, NTILE])
        step_no = sb(top, "step_no", [1, NTILE])
        base = sb(top, "base", [1, NTILE])
        spare = sb(top, "spare", [1, NTILE])
        pad_at = sb(top, "pad_at", [1, E], I32)

        made = sem("made")
        pool_settled, dve_settled = sem("pool_settled"), sem("dve_settled")
        pe_settled, sp_settled = sem("pe_settled"), sem("sp_settled")
        made_v = sem("made_v")
        image_in = [sem(f"image_in{g}") for g in range(NG)]
        tokw_in = sem("tokw_in")
        tokw_t = sem("tokw_t")
        tokw_copied = sem("tokw_copied")
        strip_t = sem("strip_t")
        strip_copied_v = sem("strip_copied_v")
        strip_copied_s = sem("strip_copied_s")
        tok_done = sem("tok_done")
        tok_biased = sem("tok_biased")
        tok_stored = [sem("tok_stored0"), sem("tok_stored1")]
        piece_in = [sem(f"piece_in{n}") for n in range(2)]
        piece_hi_set = sem("piece_hi_set")
        piece_lo = sem("piece_lo")
        b1_t = sem("b1_t")
        b1_in = sem("b1_in")
        b1_copied = sem("b1_copied")
        consts_in = sem("consts_in")
        tokb_in = sem("tokb_in")
        wqk_in = sem("wqk_in")
        wqk_set = sem("wqk_set")
        strip_set = sem("strip_set")
        spare_out = sem("spare_out")

        ones_set = sem("ones_set")
        h_in = [sem("h_in0"), sem("h_in1")]
        hd_in = sem("hd_in")
        ln1 = sem("ln1")
        rs1_set = sem("rs1_set")
        xn_set = sem("xn_set")
        xt_made = sem("xt_made")
        xt_copied = sem("xt_copied")
        qk_made = sem("qk_made")
        qk_hi = sem("qk_hi")
        qk_rest = sem("qk_rest")
        qk_mid = sem("qk_mid")
        qk_split = sem("qk_split")
        qk_out = [sem(f"qk_out{n}") for n in range(2)]
        stack_in = [[sem(f"stack_in{p}{n}") for n in range(2)] for p in range(2)]
        v_made = sem("v_made")
        v_copied = sem("v_copied")
        scores_made = sem("scores_made")
        max_taken = sem("max_taken")
        exp_done = sem("exp_done")
        sums_inverted = sem("sums_inverted")
        v_scaled = sem("v_scaled")
        pv_done = sem("pv_done")
        ctx_copied = sem("ctx_copied")
        proj_done = sem("proj_done")
        res_added = sem("res_added")
        h1_out = [sem("h1_out0"), sem("h1_out1")]
        ln2 = sem("ln2")
        rs2_set = sem("rs2_set")
        y_set = sem("y_set")
        y_hi = sem("y_hi")
        y_split = sem("y_split")
        yt_made = sem("yt_made")
        yt_copied = sem("yt_copied")
        logits_made = sem("logits_made")
        route = sem("route")
        gap_exp = sem("gap_exp")
        weigh = sem("weigh")
        rank_made = sem("rank_made")
        place = sem("place")
        rows_out = [sem("rows_out0"), sem("rows_out1")]

        b2_in = sem("b2_in")
        tab = sem("tab")
        landed_set = sem("landed_set")
        pad_idx = sem("pad_idx")
        pads_out = sem("pads_out")
        tile_in = [sem(f"tile_in{n}") for n in range(RING)]
        chain = sem("chain")
        yt2_made = sem("yt2_made")
        yt2_copied = sem("yt2_copied")
        hid_made = sem("hid_made")
        gelu_done = sem("gelu_done")
        gelu_hi = sem("gelu_hi")
        gelu_lo = sem("gelu_lo")
        tile_done = sem("tile_done")
        b2_added = sem("b2_added")
        weighted = sem("weighted")
        added = [sem(f"added{n}") for n in range(4)]

        attn = ExitStack()
        with attn:
            wqk_sb = sb(attn, "wqk_sb", [128, 2, 4, DH, HALF])
            wv_sb = sb(attn, "wv_sb", [128, 2, D])
            wo_sb = sb(attn, "wo_sb", [128, 2, D])
            router_t = sb(attn, "router_t", [DC, 2, E])
            before = sb(attn, "before", [SQ, SQ], BF16)
            ones_h = sb(attn, "ones_h", [SQ, 128], BF16)
            rev = sb(attn, "rev", [SQ, SC * E])
            rev_i = sb(attn, "rev_i", [SQ, SC * E], I32)
            token_no = sb(attn, "token_no", [SQ, SC * B], I32)
            half_neg = sb(attn, "half_neg", [SQ, SC])

            tok = ExitStack()
            with tok:
                image = [sb(tok, f"image{g}", [GR, C, P, GRID * P]) for g in range(NG)]
                strips = sb(tok, "strips", [128, 2, KTOK])
                strip = [strips[0:GR, n, :] for n in range(2)]
                tokw_nat = strips[0:DC, :, :]
                tokw = sb(tok, "tokw", [128, KC, D])
                tokb_rows = sb(tok, "tokb_rows", [GR, D])
                b1_nat = sb(tok, "b1_nat", [E * FC, 128])
                patches = [sb(tok, f"patches{n}", [128, KC, GR]) for n in range(2)]
                wq_nat, wk_nat = (p[:, :, :].rearrange("p k r -> p (k r)")[:, 0:2 * D]
                                  .rearrange("p (c h n) -> p c h n", c=2, h=H) for p in patches)
                tokens = [sb(tok, f"tokens{n}", [GR, D]) for n in range(2)]
                piece = [sb(tok, f"piece{n}", [128, F]) for n in range(2)]

            h_a = [sb(attn, f"h_a{n}", [SQ, SC, D]) for n in range(2)]
            stat1 = sb(attn, "stat1", [SQ, SC, 6])
            mv1 = sb(attn, "mv1", [SQ, SC, 2])
            ve1 = sb(attn, "ve1", [SQ, SC])
            nm1 = sb(attn, "nm1", [SQ, SC])
            rs1 = sb(attn, "rs1", [SQ, SC])
            xn = sb(attn, "xn", [SQ, SC, D])
            xt = sb(attn, "xt", [128, 2, S])
            qk_left = [sb(attn, f"qk_left{n}", [128, S]) for n in range(3)]
            qk_bits = [sb(attn, f"qk_bits{n}", [128, 3, S], BF16) for n in range(3)]
            v_raw = [sb(attn, f"v_raw{n}", [SQ, SC, H, DH]) for n in range(2)]
            q_stack = [sb(attn, f"q_stack{n}", [DC, H, S], BF16) for n in range(2)]
            k_stack = [sb(attn, f"k_stack{n}", [DC, H, S], BF16) for n in range(2)]
            probs = [sb(attn, f"probs{n}", [SQ, 4, SC, S]) for n in range(2)]
            v_over = [sb(attn, f"v_over{n}", [SQ, SC, 4, 2 * DH]) for n in range(3)]
            neg_max = sb(attn, "neg_max", [SQ, H, SC])
            sums = sb(attn, "sums", [SQ, H, SC])
            one_over = sb(attn, "one_over", [SQ, H, SC])
            ctx_t = sb(attn, "ctx_t", [128, 2, S])
            h1 = [sb(attn, f"h1_{n}", [SQ, SC, D]) for n in range(2)]
            stat2 = sb(attn, "stat2", [SQ, SC, 6])
            mv2 = sb(attn, "mv2", [SQ, SC, 2])
            ve2 = sb(attn, "ve2", [SQ, SC])
            nm2 = sb(attn, "nm2", [SQ, SC])
            rs2 = sb(attn, "rs2", [SQ, SC])
            y = sb(attn, "y", [SQ, SC, D])
            y_t = sb(attn, "y_t", [DC, 2, S])
            rows = [sb(attn, f"rows{n}", [SQ, SC, XROW], I32) for n in range(2)]
            logit = sb(attn, "logit", [SQ, SC, E])
            logit2 = sb(attn, "logit2", [SQ, SC, E])
            hit = sb(attn, "hit", [SQ, SC, E])
            first = sb(attn, "first", [SQ, SC, E])
            second = sb(attn, "second", [SQ, SC, E])
            either = sb(attn, "either", [SQ, SC, E], BF16)
            peak = sb(attn, "peak", [SQ, 4, SC])
            gap = sb(attn, "gap", [SQ, SC])
            gap_e = sb(attn, "gap_e", [SQ, SC])
            gap_1 = sb(attn, "gap_1", [SQ, SC])
            share = sb(attn, "share", [SQ, 2, SC])
            wone = sb(attn, "wone", [SQ, SC, E])
            wtwo = sb(attn, "wtwo", [SQ, SC, E])
            rank = sb(attn, "rank", [SQ, SC, E])
            at_one = sb(attn, "at_one", [SQ, SC, E])
            at_two = sb(attn, "at_two", [SQ, SC, E])
            where = [sb(attn, f"where{n}", [SQ, 2, SC], I32) for n in range(2)]

        moe = ExitStack()
        with moe:
            b2_rows = sb(moe, "b2_rows", [128, E, D])
            row_in = [sb(moe, f"row_in{n}", [128, 2, XROW], I32) for n in range(RING)]
            row_t = [sb(moe, f"row_t{n}", [128, 3, TILE], BF16) for n in range(2)]
            gelu = [sb(moe, f"gelu{n}", [128, FC * TILE]) for n in range(2)]
            g_hi = [sb(moe, f"g_hi{n}", [128, FC * TILE], BF16) for n in range(2)]
            g_lo = [sb(moe, f"g_lo{n}", [128, FC * TILE], BF16) for n in range(2)]
            with_b2 = sb(moe, "with_b2", [128, 2, D])
            result = [sb(moe, f"result{n}", [128, 2, D]) for n in range(4)]

        past, past_n = (p[0:1, 0:3, :, :].rearrange("o a c q -> o (a c q)")[:, 0:NTILE * E]
                        .rearrange("o (j e) -> o j e", e=E) for p in probs)

        SCORE, PV, MC, MA = bank[0:4], bank[4], bank[5], bank[6:8]
        patch_ps = [bank[0:2], bank[2:4]]
        tok_ps = bank[4:6]
        b1_ps = bank[6]
        hid_ps = [bank[0:3], bank[3:6]]
        rowt_ps, tile_ps = bank[6], bank[7]

        NSTEP = NG * GRID
        LOADS_AHEAD = 4
        NPIECE = 4 * E

        def pieces_of(n):
            return [m for m in range(NPIECE) if m * NSTEP // NPIECE == n]

        def batches(eng, body):
            for i in range(-1, 4):
                body(Step(i // 2, i % 2, 2), lambda n, i=i: 0 <= i + n < B)
            last = B - 4
            if last > 4:
                with eng.Fori(2, last // 2) as turn:
                    for k in range(2):
                        body(Step(turn, k, 2), lambda n: True)
            for i in range(last, B + 3):
                body(Step(i // 2, i % 2, 2), lambda n, i=i: 0 <= i + n < B)

        def first_iteration(body):
            body(Step(-1, 0, 2), lambda n: 0 <= n - 2 < B)

        def expert_tiles(eng, body):
            for j in range(RING):
                body(Step(0, j, RING), lambda n, j=j: 0 <= j + n < NTILE)
            with eng.Fori(1, NTILE // RING - 1) as turn:
                for k in range(RING):
                    body(Step(turn, k, RING), lambda n: True)
            for j in range(NTILE - RING, NTILE + 1):
                body(Step(j // RING, j % RING, RING), lambda n, j=j: 0 <= j + n < NTILE)

        def small_bank(n, has):
            return MC if has(0) else SCORE[n]

        block = top.enter_context(nc.Block())

        @block.sync
        def _(sp):
            sp.dma_start(tokw_nat[:, :, :], tok_w.rearrange("(c p) k -> p c k", p=DC)).then_inc(tokw_in, 16)

            def load_image(g, n):
                sp.dma_start(image[g][GRID * n:GRID * n + GRID, :, :, :].rearrange("r c y x -> r c (y x)"),
                             x[g * GB + n, :, :, :].rearrange("c (r y) x -> r c (y x)", y=P)).then_inc(image_in[g], 16)

            def load_constant(n):
                if n < H:
                    at = WO_AT[n][1]
                    sp.dma_start(wo_sb[at:at + DH, WO_AT[n][0], :], wo[DH * n:DH * n + DH, :]).then_inc(consts_in, 16)
                elif n == H:
                    sp.dma_start(wo_sb[BO_ROW:BO_ROW + 1, 1, :], bo.rearrange("(a n) -> a n", a=1)).then_inc(consts_in, 16)
                elif n == H + 1:
                    sp.dma_start(wv_sb[:, 0, :].rearrange("p (h n) -> p h n", n=DH),
                                 wv[:, 0:128, :].rearrange("h p n -> p h n")).then_inc(consts_in, 16)
                elif n == H + 2:
                    sp.dma_start(wv_sb[0:ONES, 1, :].rearrange("p (h n) -> p h n", n=DH),
                                 wv[:, 128:D, :].rearrange("h p n -> p h n")).then_inc(consts_in, 16)
                elif n == H + 3:
                    sp.dma_start(wv_sb[ONES:ONES + 1, 1, :], bv.rearrange("(a h) n -> a (h n)", a=1)).then_inc(consts_in, 16)
                else:
                    c = n - H - 4
                    with nc.allow_non_contiguous_dma(reason="1,536 weights of the router, transposed"):
                        sp.dma_start(router_t[:, c, :], router[:, DC * c:DC * c + DC].rearrange("e p -> p e")).then_inc(consts_in, 16)

            for n in range(GB):
                load_image(0, n)
            sp.wait_ge(made_v, 2)

            def load_tokens(dst, b, done):
                pr = patch_rows.rearrange("(b n) d -> b n d", n=NPATCH)
                one = bass.ds(b.i, 1)
                rest = NPATCH - SQ
                sp.dma_start(dst[:, 0, :], pr[one, 0:SQ, :].rearrange("a n d -> (a n) d")).then_inc(done, 16)
                sp.dma_start(dst[0:rest, 1, :], pr[one, SQ:NPATCH, :].rearrange("a n d -> (a n) d")).then_inc(done, 16)
                sp.dma_start(dst[rest:SQ, 1, :], txt[one, 0:SQ - rest, :].rearrange("a n d -> (a n) d")).then_inc(done, 16)
                sp.dma_start(dst[:, 2, :], txt[one, SQ - rest:NTEXT, :].rearrange("a n d -> (a n) d")).then_inc(done, 16)

            def load_stack(b, half):
                sp.wait_ge(qk_out[half], 48 * b.i + 48)
                settle(sp, sp_settled)
                wait(sp, scores_made, 36 * b.i - 54 + 18 * half)
                o = b.odd
                hs = slice(HALF * half, HALF * half + HALF)
                for part, p0, copies in STACK_Q:
                    for n in range(copies):
                        src = qk_parts[o, 2 * half, part * DC:(part + 1) * DC, :].rearrange("(d h) q -> d (h q)", h=HALF)
                        sp.dma_start(q_stack[o][p0 + 16 * n:p0 + 16 * n + 16, hs, :].rearrange("p h q -> p (h q)"), src)\
                            .then_inc(stack_in[o][half], 16)
                for part, p0, parts in STACK_K:
                    src = qk_parts[o, 2 * half + 1, part * DC:(part + parts) * DC, :].rearrange("(d h) q -> d (h q)", h=HALF)
                    sp.dma_start(k_stack[o][p0:p0 + 16 * parts, hs, :].rearrange("p h q -> p (h q)"), src)\
                        .then_inc(stack_in[o][half], 16)

            def store_parts(b, n, half):
                for which, r0, p0, rows_ in QK_TILES[n]:
                    if which // 2 == half:
                        sp.wait_ge(qk_split, 3 * b.i + n + 1)
                        sp.dma_start(qk_parts[b.odd, which, :, :].rearrange("(c r) q -> r c q", c=3)[r0:r0 + rows_, :, :],
                                     qk_bits[n][p0:p0 + rows_, :, :]).then_inc(qk_out[half], 16)

            def iteration(i, has):
                a, c_, d_ = i + 1, i, i + -1
                if has(3):
                    up = i + 3
                    wait(sp, xn_set, SC * (up.i - 1))
                    load_tokens(h_a[up.odd], up, h_in[up.odd])
                if has(1):
                    store_parts(a, 0, 0)
                    store_parts(a, 1, 0)
                if has(-1):
                    sp.wait_ge(res_added, SC * d_.i + SC)
                    sp.dma_start(out[bass.ds(S * d_.i, S), :].rearrange("(c p) d -> p c d", p=SQ),
                                 h1[d_.odd][:, :, :]).then_inc(h1_out[d_.odd], 16)
                if has(1):
                    load_stack(a, 0)
                if has(0):
                    wait(sp, h1_out[c_.odd], 16 * c_.turn)
                    settle(sp, sp_settled)
                    wait(sp, y_set, SC * c_.i - SC)
                    load_tokens(h1[c_.odd], c_, hd_in)
                if has(1):
                    store_parts(a, 1, 1)
                    store_parts(a, 2, 1)
                    load_stack(a, 1)
            column = patch_rows.rearrange("(r x) d -> r x d", x=GRID)
            for n in range(NSTEP):
                g, gx = n // GRID, n % GRID
                sp.wait_ge(tok_biased, n + 1)
                sp.dma_start(column[g * GR:(g + 1) * GR, gx, :], tokens[n % 2][:, :]).then_inc(tok_stored[n % 2], 16)
                if gx < GB and g + 1 < NG:
                    load_image(g + 1, gx)
                for k in range(n * NCONST // NSTEP, (n + 1) * NCONST // NSTEP):
                    load_constant(k)
                if n == NSTEP - LOADS_AHEAD:
                    for k in range(2):
                        sp.wait_ge(tok_stored[k], 16 * (GRID // 2))
                    sp.wait_ge(strip_set, GRID)
                    load_tokens(h_a[0], Step(0, 0, 2), h_in[0])
                    first_iteration(iteration)
            for n in range(2):
                sp.wait_ge(tok_stored[n], 16 * (NSTEP // 2))

            batches(sp, iteration)

            sp.wait_ge(pad_idx, 1)
            for e in range(E):
                end = sp.value_load(pad_at[0:1, e:e + 1], min_val=e * REGION, max_val=e * REGION + NTOK)
                sp.dma_start(expert_rows[bass.ds(end, TILE), :].rearrange("(u p) w -> p u w", u=2),
                             pad_rows[:, :, :]).then_inc(pads_out, 16)
            sp.wait_ge(tab, 1)
            sp.wait_ge(pads_out, 16 * E)
            sp.wait_ge(spare_out, 16 * NSPARE)
            for n in range(2):
                sp.wait_ge(rows_out[n], 96 * (B // 2))
                sp.wait_ge(h1_out[n], 16 * (B // 2))

            def tile(j, has):
                if has(0):
                    if not (isinstance(j.turn, int) and j.turn == 0):
                        sp.wait_ge(added[j.slot % 4], 32 * (j.fours() - 1) + 16)
                    row = sp.value_load(tile_row[0:1, bass.ds(j.i, 1)], min_val=0,
                                        max_val=E * REGION + (NSPARE - 1) * TILE)
                    sp.dma_start(row_in[j.slot][:, :, :], expert_rows[bass.ds(row, TILE), :]
                                 .rearrange("(u p) w -> p u w", u=2)).then_inc(tile_in[j.slot], 16)
                    if isinstance(j.turn, int) and j.i == 1:
                        sp.dma_start(b2_rows[:, :, :].rearrange("p e n -> p (e n)"),
                                     b2.rearrange("(a e) n -> a (e n)", a=1).to_broadcast([128, E * D])).then_inc(b2_in, 16)

            expert_tiles(sp, tile)
            for n in range(4):
                sp.wait_ge(added[n], 32 * (NTILE // 4) + 16)

        @block.gpsimd
        def _(pool):
            g = nc.gpsimd
            g.memset(ident[:, :], 0.0).then_inc(made, 1)
            g.memset(before[:, :], 1.0).then_inc(made, 1)
            g.iota(rev_i[:, :], [[0, SC], [-1, E]], base=E, channel_multiplier=0).then_inc(made, 1)
            g.iota(tile_no_i[:, :], [[1, NTILE]], base=0, channel_multiplier=0).then_inc(made, 1)
            g.iota(token_no[:, :], [[SQ, SC * B]], base=0, channel_multiplier=1).then_inc(made, 1)
            g.memset(pad_rows[:, :, :], 0).then_inc(made, 1)
            g.memset(half_neg[:, :], -0.5).then_inc(made, 1)
            pool.wait_ge(made, 7)
            g.affine_select(out=ident[:, :], in_=ident[:, :], compare_op=ALU.not_equal, fill=1.0, base=0,
                            pattern=[[-1, 128]], channel_multiplier=1).then_inc(made, 1)
            g.affine_select(out=before[:, :], in_=before[:, :], compare_op=ALU.is_gt, fill=0.0, base=0,
                            pattern=[[1, SQ]], channel_multiplier=-1).then_inc(made, 1)
            g.iota(pad_rows[:, :, TOKEN], [[128, 2]], base=NTOK,
                   channel_multiplier=1).then_inc(made, 1)
            pool.wait_ge(made, 10)
            pool.wait_ge(made_v, 1)
            for n in range(NSPARE):
                pool.dma_start(expert_rows[E * REGION + TILE * n:E * REGION + TILE * n + TILE, :]
                               .rearrange("(u p) w -> p u w", u=2), pad_rows[:, :, :]).then_inc(spare_out, 16)
            for n in range(4):
                at = NTOK + TILE // 4 * n
                pool.dma_start(out[at:at + TILE // 4, :], pad_rows[0:TILE // 4, 0, 0:D].bitcast(F32)).then_inc(added[n], 16)

            def norm(b, src, stat_set, per, ve, nm, rs, rs_set, dst, dst_set, dst_free):
                pool.wait_ge(stat_set, per * b.i + per)
                g.tensor_tensor(rs[:, :], ve[:, :], half_neg[:, :], ALU.pow).then_inc(rs_set, 1)
                pool.wait_ge(rs_set, b.i + 1)
                for sem_, value in dst_free:
                    wait(pool, sem_, value)
                settle(pool, pool_settled)
                for c in range(SC):
                    g.tensor_scalar(dst[:, c, :], src[:, c, :], nm[:, c:c + 1], rs[:, c:c + 1],
                                    ALU.add, ALU.mult).then_inc(dst_set, 1)

            def split(b, n):
                pool.wait_ge(qk_rest, 3 * b.i + n + 1)
                settle(pool, pool_settled)
                g.tensor_copy(qk_bits[n][:, 1, :], qk_left[n][:, :]).then_inc(qk_mid, 1)
                pool.wait_ge(qk_mid, 3 * b.i + n + 1)
                g.tensor_tensor(qk_bits[n][:, 2, :], qk_left[n][:, :], qk_bits[n][:, 1, :], ALU.subtract).then_inc(qk_split, 1)

            def iteration(i, has):
                up, a, d_, f_ = i + 2, i + 1, i + -1, i + -3
                if has(-3):
                    pool.wait_ge(place, PLACE * f_.i + PLACE)
                    pool.wait_ge(weigh, 6 * f_.i + 6)
                    settle(pool, pool_settled)
                    for c in range(SC):
                        for slot in range(2):
                            g.indirect_dma_start(
                                out=expert_rows[:, :],
                                out_offset=bass.IndirectOffsetOnAxis(where[f_.odd][:, slot, c:c + 1], 0),
                                in_=rows[f_.odd][:, c, :], in_offset=None).then_inc(rows_out[f_.odd], 16)
                if has(2):
                    norm(up, h_a[up.odd], ln1, 8, ve1, nm1, rs1, rs1_set, xn, xn_set,
                         [(xt_made, 2 * up.i)])
                if has(1):
                    split(a, 0)
                    split(a, 1)
                if has(-1):
                    norm(d_, h1[d_.odd], ln2, 8, ve2, nm2, rs2, rs2_set, y, y_set,
                         [(yt_made, 2 * d_.i), (y_split, 3 * d_.i)])
                if has(1):
                    split(a, 2)
                if has(-1):
                    pool.wait_ge(y_hi, d_.i + 1)
                    r = rows[d_.odd][:, :, 0:YWORDS].bitcast(BF16)
                    g.tensor_tensor(r[:, :, D:D + 64], y[:, :, 128:D], r[:, :, 128:D], ALU.subtract).then_inc(y_split, 1)
                    g.tensor_tensor(r[:, :, D + 64:2 * D], y[:, :, 0:128], r[:, :, 0:128], ALU.subtract).then_inc(y_split, 1)
                    g.tensor_copy(rows[d_.odd][:, :, TOKEN],
                                  token_no[:, bass.ds(SC * d_.i, SC)]).then_inc(y_split, 1)

            for n in range(NSTEP):
                gr, gx = n // GRID, n % GRID
                if gx == 0:
                    pool.wait_ge(image_in[gr], 16 * GB)
                wait(pool, strip_t, n - 1)
                if n == 0:
                    pool.wait_ge(tokw_t, 3)
                g.tensor_copy(strip[n % 2].rearrange("r (k x) -> r k x", x=P),
                              image[gr][:, :, :, P * gx:P * gx + P].rearrange("r c y x -> r (c y) x")).then_inc(strip_set, 1)

            first_iteration(iteration)
            pool.wait_ge(ones_set, 1)
            pool.wait_ge(consts_in, 16 * NCONST)

            batches(pool, iteration)

            pool.wait_ge(landed_set, 1)
            pool.wait_ge(spare_out, 16 * NSPARE)
            for n in range(2):
                pool.wait_ge(h1_out[n], 16 * (B // 2))

            def tile(j, has):
                if has(-1):
                    t = j + -1
                    landed = [pool.value_load(tile_land[0:1, n, bass.ds(t.i, 1)], min_val=16, max_val=32 * NTILE + 16)
                              for n in range(4)]
                    for n in range(4):
                        pool.wait_ge(added[n], landed[n])
                    pool.wait_ge(weighted, t.i + 1)
                    settle(pool, pool_settled)
                    for u in range(2):
                        g.indirect_dma_start(
                            out=out[:, :],
                            out_offset=bass.IndirectOffsetOnAxis(row_in[t.slot][:, u, TOKEN:TOKEN + 1], 0),
                            in_=result[t.slot % 4][:, u, :], in_offset=None, compute_op=ALU.add).then_inc(added[t.slot % 4], 16)

            expert_tiles(pool, tile)

        @block.scalar
        def _(act):
            s = nc.scalar
            act.dma_start(tokb_rows[:, :], tok_b.rearrange("(a n) -> a n", a=1).to_broadcast([GR, D])).then_inc(tokb_in, 16)
            act.dma_start(b1_nat[:, :], b1.rearrange("e (f p) -> (e f) p", p=128)).then_inc(b1_in, 16)
            for dst, w, bias in ((wq_nat, wq, bq), (wk_nat, wk, bk)):
                act.dma_start(dst[:, 0, :, :], w[:, 0:128, :].rearrange("h p n -> p h n")).then_inc(wqk_in, 16)
                act.dma_start(dst[0:ONES, 1, :, :], w[:, 128:D, :].rearrange("h p n -> p h n")).then_inc(wqk_in, 16)
                act.dma_start(dst[ONES:ONES + 1, 1, :, :].rearrange("o h n -> o (h n)"),
                              bias.rearrange("(a h) n -> a (h n)", a=1)).then_inc(wqk_in, 16)

            def load_piece(n):
                e, k = divmod(n, 4)
                dst = piece[n % 2]
                wait(act, piece_lo, n - 1)
                wait(act, piece_hi_set, n - 1)
                done = piece_in[n % 2]
                if k == 0:
                    act.dma_start(dst[:, :], w1[e, 0:128, :]).then_inc(done, 32)
                elif k == 1:
                    act.dma_start(dst[0:64, :], w1[e, 128:D, :]).then_inc(done, 16)
                    act.dma_start(dst[64:128, :], w1[e, 128:D, :]).then_inc(done, 16)
                else:
                    f = 3 * (k - 2)
                    act.dma_start(dst[:, 0:3 * D].rearrange("p (c n) -> p c n", c=3),
                                  w2[e, 128 * f:128 * f + 384, :].rearrange("(c p) n -> p c n", p=128)).then_inc(done, 32)

            def split_hi(n):
                e, k = divmod(n, 4)
                src = piece[n % 2]
                act.wait_ge(piece_in[n % 2], 32 * (n // 2) + 32)
                if k < 2:
                    s.activation(w1_parts[:, e, (HI_A, HI_B)[k], :], src[:, :], ACT.Copy).then_inc(piece_hi_set, 1)
                else:
                    f = 3 * (k - 2)
                    s.activation(w2_hi[:, e, f:f + 3, :].rearrange("p c n -> p (c n)"), src[:, 0:3 * D], ACT.Copy)\
                        .then_inc(piece_hi_set, 1)

            load_piece(0)
            load_piece(1)
            act.wait_ge(b1_t, 1)
            s.activation(b1_cols[:, :], b1_ps[:, 0:E * FC], ACT.Copy).then_inc(b1_copied, 1)
            act.wait_ge(wqk_set, 8)
            for n in range(NSTEP + 1):
                if n < NSTEP:
                    act.wait_ge(strip_t, n + 1)
                    if n >= 2:
                        act.wait_ge(tok_done, n - 1)
                    s.activation(patches[n % 2][:, 3:6, :].rearrange("p c r -> p (c r)"),
                                 patch_ps[n % 2][1][:, 0:3 * GR], ACT.Copy).then_inc(strip_copied_s, 1)
                for m in pieces_of(n):
                    split_hi(m)
                    if m + 2 < NPIECE:
                        load_piece(m + 2)

            act.wait_ge(ones_set, 1)

            def copy_ctx(b, n):
                act.wait_ge(pv_done, 3 * b.i + 2 + n)
                if n == 0:
                    wait(act, proj_done, SC * b.i)
                    s.activation(ctx_t[:, 0, :], PV[:, 0:S], ACT.Copy).then_inc(ctx_copied, 1)
                else:
                    s.activation(ctx_t[:, 1, :], PV[:, 0:S], ACT.Identity,
                                 bias=ident[:, BO_ROW:BO_ROW + 1]).then_inc(ctx_copied, 1)

            def iteration(i, has):
                a, c_, d_, e_ = i + 1, i, i + -1, i + -2
                for t in range(H * SC):
                    h = t // SC
                    if has(0):
                        grp, j = h // 4, h % 4
                        if t % 12 == 0:
                            wait(act, pv_done, 3 * c_.i + grp - 1)
                        act.wait_ge(max_taken, 36 * c_.i + t + 1)
                        s.activation(probs[(c_.odd + grp) % 2][:, j, t % SC, :], SCORE[t % 4][0:SQ, 0:S],
                                     ACT.Exp, bias=neg_max[:, h, t % SC:t % SC + 1],
                                     accum_out=sums[:, h, t % SC:t % SC + 1]).then_inc(exp_done, 1)
                    if t in (1, 11) and has(-1):
                        copy_ctx(d_, t // 11)
                    if t in (0, 2) and has(1):
                        n = t // 2
                        act.wait_ge(xt_made, 2 * a.i + n + 1)
                        wait(act, v_made, 2 * a.i)
                        rows_ = (128, ONES)[n]
                        s.activation(xt[0:rows_, n, :], MA[n][0:rows_, 0:S], ACT.Copy).then_inc(xt_copied, 1)
                    if t in (6, 10, 22) and has(1):
                        n = (6, 10, 22).index(t)
                        act.wait_ge(qk_made, 3 * a.i + n + 1)
                        if n < 2:
                            wait(act, qk_out[n], 48 * a.i)
                        s.activation(qk_bits[n][:, 0, :], MA[n % 2][:, 0:S], ACT.Copy).then_inc(qk_hi, 1)
                    if t == 18 and has(-2):
                        act.wait_ge(route, ROUTE * e_.i + ROUTE)
                        s.activation(gap_e[:, :], gap[:, :], ACT.Exp).then_inc(gap_exp, 1)
                    if t in (27, 30) and has(1):
                        n = (t - 27) // 3
                        nchunk = 2 - n
                        act.wait_ge(v_made, 2 * a.i + n + 1)
                        wait(act, v_scaled, 3 * a.i - 3)
                        s.activation(v_raw[a.odd][:, 2 * n:2 * n + nchunk, :, :].rearrange("p c h n -> p (c h n)"),
                                     MA[1 - n][0:SQ, 0:nchunk * D], ACT.Copy).then_inc(v_copied, 1)
                    if t in (32, 34) and has(-1):
                        n = (t - 32) // 2
                        act.wait_ge(yt_made, 2 * d_.i + n + 1)
                        wait(act, logits_made, d_.i)
                        s.activation(y_t[:, n, :], small_bank(n, has)[0:DC, 0:S], ACT.Copy).then_inc(yt_copied, 1)
                    if t == (33 if has(0) else 35) and has(-1):
                        act.wait_ge(y_set, SC * d_.i + SC)
                        wait(act, rows_out[d_.odd], 96 * d_.turn)
                        s.activation(rows[d_.odd][:, :, 0:YWORDS].bitcast(BF16)[:, :, 0:D], y[:, :, :], ACT.Copy)\
                            .then_inc(y_hi, 1)

            batches(act, iteration)

            s.activation(gelu_table[:, :], ident[:, 0:1], ACT.Gelu)
            act.wait_ge(tab, 1)

            def copy_rows(j):
                act.wait_ge(yt2_made, j.i + 1)
                wait(act, hid_made, 3 * (j.i - 1))
                s.activation(row_t[j.odd][:, :, :].rearrange("p c n -> p (c n)"),
                             rowt_ps[:, :].bitcast(BF16)[:, 0:3 * TILE], ACT.Copy).then_inc(yt2_copied, 1)

            def tile(j, has):
                if has(0):
                    e = act.value_load(tile_expert[0:1, bass.ds(j.i + 4, 1)], min_val=0, max_val=E - 1)
                if has(1):
                    copy_rows(j + 1)
                if has(0):
                    for f in range(FC):
                        if f % 2 == 0:
                            act.wait_ge(hid_made, 3 * j.i + f // 2 + 1)
                            wait(act, gelu_lo, 3 * (j.i - 2) + f // 2 + 1)
                        last = s.activation(gelu[j.odd][:, TILE * f:TILE * f + TILE],
                                            hid_ps[j.odd][f // 2][:, TILE * (f % 2):TILE * (f % 2) + TILE],
                                            ACT.Gelu, bias=b1_cols[:, bass.ds(FC * e + f, 1)])
                        if f % 2 == 1:
                            last.then_inc(gelu_done, 1)

            copy_rows(Step(0, 0, RING))
            expert_tiles(act, tile)

        @block.vector
        def _(dve):
            v = nc.vector
            dve.wait_ge(made, 10)
            v.tensor_copy(ident_h[:, :], ident[:, :]).then_inc(made_v, 1)
            v.memset(wo_sb[:, :, :], 0.0).then_inc(made_v, 1)
            v.memset(ones_h[:, :], 1.0).then_inc(made_v, 1)
            v.tensor_copy(rev[:, :], rev_i[:, :]).then_inc(made_v, 1)
            v.memset(w1_parts[64:128, :, LO_B, :], 0.0).then_inc(made_v, 1)
            for e in range(E):
                v.memset(carry[:, e:e + 1], float(e * REGION))
                v.memset(region[:, e:e + 1], e * REGION - (TILE - 1.0)).then_inc(made_v, 1)
            v.memset(tile_expert[:, 0:4], 0)
            v.tensor_copy(tile_no[:, :], tile_no_i[:, :]).then_inc(made_v, 1)
            for n in range(3):
                dve.wait_ge(tokw_t, n + 1)
                v.tensor_copy(tokw[:, 2 * n:2 * n + 2, :].rearrange("p c n -> p (c n)"),
                              bank[n][:, 0:2 * D]).then_inc(tokw_copied, 1)

            def split_lo(n):
                e, k = divmod(n, 4)
                src = piece[n % 2]
                dve.wait_ge(piece_hi_set, n + 1)
                if k == 0:
                    v.tensor_tensor(w1_parts[:, e, LO_A, :], src[:, :], w1_parts[:, e, HI_A, :], ALU.subtract).then_inc(piece_lo, 1)
                elif k == 1:
                    v.tensor_tensor(w1_parts[0:64, e, LO_B, :], src[0:64, :], w1_parts[0:64, e, HI_B, :],
                                    ALU.subtract).then_inc(piece_lo, 1)
                else:
                    f = 3 * (k - 2)
                    v.tensor_tensor(w2_lo[:, e, f:f + 3, :].rearrange("p c n -> p (c n)"), src[:, 0:3 * D],
                                    w2_hi[:, e, f:f + 3, :].rearrange("p c n -> p (c n)"), ALU.subtract).then_inc(piece_lo, 1)

            def row_statistics(b, stat, mv, done):
                dve.wait_ge(done, 8 * b.i + 3)
                settle(dve, dve_settled)
                for c in range(SC):
                    v.bn_aggr(mv[:, c, :], stat[:, c, :]).then_inc(done, 1)

            def variance_and_mean(b, mv, ve, nm, done):
                dve.wait_ge(done, 8 * b.i + 6)
                v.tensor_scalar(ve[:, :], mv[:, :, 1], EPS, None, ALU.add).then_inc(done, 1)
                v.tensor_scalar(nm[:, :], mv[:, :, 0], -1.0, None, ALU.mult).then_inc(done, 1)

            def scale_v(b, grp):
                hs = slice(4 * grp, 4 * grp + 4)
                dve.wait_ge(exp_done, 36 * b.i + 12 * grp + 12)
                v.reciprocal(one_over[:, hs, :].rearrange("p j c -> p (j c)"),
                             sums[:, hs, :].rearrange("p j c -> p (j c)")).then_inc(sums_inverted, 1)
                if grp == 0:
                    dve.wait_ge(v_copied, 2 * b.i + 2)
                wait(dve, pv_done, 3 * b.i + grp - 2)
                dve.wait_ge(sums_inverted, 3 * b.i + grp + 1)
                at = DH * (grp % 2)
                for c in range(SC):
                    last = v.tensor_tensor(v_over[grp][:, c, :, at:at + DH], v_raw[b.odd][:, c, hs, :],
                                           one_over[:, hs, c:c + 1].to_broadcast([SQ, 4, DH]), ALU.mult)
                last.then_inc(v_scaled, 1)

            def bc(t):
                return t.rearrange("p (c o) -> p c o", o=1).to_broadcast([SQ, SC, E])

            def flat(t):
                return t[:, :, :].rearrange("p c e -> p (c e)")

            def choose(b, n):
                src, hot, m = (logit, first, 0) if n < 6 else (logit2, second, 1)
                if n == 0:
                    dve.wait_ge(logits_made, b.i + 1)
                    wait(dve, weigh, 6 * b.i)
                    ins = v.tensor_copy(flat(logit), MC[0:SQ, 0:SC * E])
                else:
                    dve.wait_ge(route, ROUTE * b.i + n)
                if n in (1, 7):
                    ins = v.tensor_reduce(peak[:, 2 * m, :], src[:, :, :], AX.X, ALU.max)
                if n in (2, 8):
                    ins = v.tensor_tensor(hit[:, :, :], src[:, :, :], bc(peak[:, 2 * m, :]), ALU.is_ge)
                if n in (3, 9):
                    ins = v.tensor_tensor(flat(hit), flat(hit), rev[:, :], ALU.mult)
                if n in (4, 10):
                    ins = v.tensor_reduce(peak[:, 2 * m + 1, :], hit[:, :, :], AX.X, ALU.max)
                if n in (5, 11):
                    ins = v.tensor_tensor(hot[:, :, :], hit[:, :, :], bc(peak[:, 2 * m + 1, :]), ALU.is_equal)
                if n == 6:
                    ins = v.scalar_tensor_tensor(flat(logit2), flat(first), -3e38, flat(logit), ALU.mult, ALU.add)
                if n == 12:
                    ins = v.tensor_tensor(either[:, :, :], first[:, :, :], second[:, :, :], ALU.add)
                if n == 13:
                    ins = v.tensor_tensor(gap[:, :], peak[:, 2, :], peak[:, 0, :], ALU.subtract)
                ins.then_inc(route, 1)

            def weights(b, n):
                if n == 0:
                    dve.wait_ge(gap_exp, b.i + 1)
                    ins = v.tensor_scalar(gap_1[:, :], gap_e[:, :], 1.0, None, ALU.add)
                else:
                    dve.wait_ge(weigh, 6 * b.i + n)
                if n == 1:
                    ins = v.reciprocal(share[:, 0, :], gap_1[:, :])
                if n == 2:
                    ins = v.tensor_tensor(share[:, 1, :], gap_e[:, :], share[:, 0, :], ALU.mult)
                if n == 3:
                    ins = v.tensor_tensor(wone[:, :, :], first[:, :, :], bc(share[:, 0, :]), ALU.mult)
                if n == 4:
                    ins = v.tensor_tensor(wtwo[:, :, :], second[:, :, :], bc(share[:, 1, :]), ALU.mult)
                if n == 5:
                    dve.wait_ge(y_split, 3 * b.i + 3)
                    ins = v.tensor_tensor(rows[b.odd][:, :, YWORDS:TOKEN].bitcast(F32), wone[:, :, :], wtwo[:, :, :], ALU.add)
                ins.then_inc(weigh, 1)

            def places(b, n):
                if n == 0:
                    dve.wait_ge(rank_made, b.i + 1)
                    ins = v.tensor_tensor(rank[:, :, :], MC[0:SQ, 0:SC * E].rearrange("p (c e) -> p c e", c=SC),
                                          carry[0:SQ, :].rearrange("p (o e) -> p o e", o=1).to_broadcast([SQ, SC, E]), ALU.add)
                else:
                    dve.wait_ge(place, PLACE * b.i + n)
                if n == 1:
                    ins = v.tensor_tensor(carry[:, :], MC[:, SC * E:SC * E + E], carry[:, :], ALU.add)
                if n == 2:
                    v.tensor_tensor(at_one[:, :, :], first[:, :, :], rank[:, :, :], ALU.mult)
                    ins = v.tensor_tensor(at_two[:, :, :], second[:, :, :], rank[:, :, :], ALU.mult)
                if n == 3:
                    wait(dve, rows_out[b.odd], 96 * b.turn)
                    with nc.allow_low_precision(reason="one of the 8 summands is a row number, the others are 0"):
                        v.tensor_reduce(where[b.odd][:, 0, :], at_one[:, :, :], AX.X, ALU.add)
                        ins = v.tensor_reduce(where[b.odd][:, 1, :], at_two[:, :, :], AX.X, ALU.add)
                ins.then_inc(place, 1)

            def iteration(i, has):
                up, a, c_, d_, e_ = i + 2, i + 1, i, i + -1, i + -2
                for t in range(H * SC):
                    if has(0):
                        dve.wait_ge(scores_made, 36 * c_.i + t + 1)
                        v.tensor_reduce(neg_max[:, t // SC, t % SC:t % SC + 1], SCORE[t % 4][0:SQ, 0:S],
                                        AX.X, ALU.max, negate=True).then_inc(max_taken, 1)
                    if t in (0, 1, 2) and has(2):
                        dve.wait_ge(h_in[up.odd], 64 * up.turn + 64)
                        if t == 0:
                            wait(dve, rs1_set, up.i)
                            wait(dve, xn_set, SC * up.i)
                        v.bn_stats(stat1[:, t, :], h_a[up.odd][:, t, :]).then_inc(ln1, 1)
                    if t == 5 and has(2):
                        row_statistics(up, stat1, mv1, ln1)
                    if t == 6 and has(2):
                        variance_and_mean(up, mv1, ve1, nm1, ln1)
                    if t == 3 and has(-1):
                        scale_v(d_, 2)
                    if 4 <= t < 4 + ROUTE and has(-2):
                        choose(e_, t - 4)
                    if t == 15 and has(0):
                        scale_v(c_, 0)
                    if t == 27 and has(0):
                        scale_v(c_, 1)
                    if t in (16, 18, 21) and has(-1):
                        c = (16, 18, 21).index(t)
                        dve.wait_ge(proj_done, SC * d_.i + c + 1)
                        if c == 0:
                            dve.wait_ge(hd_in, 64 * d_.i + 64)
                        v.tensor_tensor(h1[d_.odd][:, c, :], small_bank(c, has)[0:SQ, 0:D], h1[d_.odd][:, c, :], ALU.add).then_inc(res_added, 1)
                    if t in (17, 19, 22) and has(-1):
                        c = (17, 19, 22).index(t)
                        dve.wait_ge(res_added, SC * d_.i + c + 1)
                        v.bn_stats(stat2[:, c, :], h1[d_.odd][:, c, :]).then_inc(ln2, 1)
                    if t == 23 and has(-1):
                        wait(dve, rs2_set, d_.i)
                        wait(dve, y_set, SC * d_.i)
                        row_statistics(d_, stat2, mv2, ln2)
                    if t == 24 and has(-1):
                        variance_and_mean(d_, mv2, ve2, nm2, ln2)
                    if t in (10, 14, 26) and has(1):
                        n = (10, 14, 26).index(t)
                        dve.wait_ge(qk_hi, 3 * a.i + n + 1)
                        wait(dve, qk_split, 3 * (a.i - 1) + n + 1)
                        v.tensor_tensor(qk_left[n][:, :], MA[n % 2][:, 0:S], qk_bits[n][:, 0, :], ALU.subtract)\
                            .then_inc(qk_rest, 1)
                    if 20 <= t < 26 and has(-2):
                        weights(e_, t - 20)
                    if 28 <= t < 28 + PLACE and has(-2):
                        places(e_, t - 28)

            dve.wait_ge(wqk_in, 16 * 6)
            for k, src in enumerate((wq_nat, wk_nat)):
                for c in range(2):
                    for half in range(2):
                        v.tensor_scalar(wqk_sb[0:XK[c], c, 2 * half + k, :, :],
                                        src[0:XK[c], c, HALF * half:HALF * half + HALF, :].rearrange("p h n -> p n h"),
                                        1.0 if k else float(DH) ** -0.5, None, ALU.mult).then_inc(wqk_set, 1)
            dve.wait_ge(wqk_set, 8)
            dve.wait_ge(tokb_in, 16)
            for n in range(NSTEP + 1):
                if n < NSTEP:
                    dve.wait_ge(strip_t, n + 1)
                    if n >= 2:
                        dve.wait_ge(tok_done, n - 1)
                    v.tensor_copy(patches[n % 2][:, 0:3, :].rearrange("p c r -> p (c r)"),
                                  patch_ps[n % 2][0][:, 0:3 * GR]).then_inc(strip_copied_v, 1)
                if n >= 1:
                    dve.wait_ge(tok_done, n)
                    wait(dve, tok_stored[(n - 1) % 2], 16 * ((n - 1) // 2))
                    v.tensor_tensor(tokens[(n - 1) % 2][:, :], tok_ps[(n - 1) % 2][0:GR, 0:D], tokb_rows[:, :], ALU.add).then_inc(tok_biased, 1)
                for m in pieces_of(n):
                    split_lo(m)
                if n == NSTEP - 2:
                    first_iteration(iteration)
                    v.memset(xt[ONES:ONES + 1, 1, :], 1.0).then_inc(ones_set, 1)

            dve.wait_ge(tok_done, NSTEP)
            for n in range(2):
                dve.wait_ge(tok_stored[n], 16 * (NSTEP // 2))
            for n in range(3):
                v.memset(v_over[n][:, :, :, :], 0.0)

            batches(dve, iteration)

            k = [0]

            def link(ins):
                k[0] += 1
                ins.then_inc(chain, 1)
                dve.wait_ge(chain, k[0])

            dve.wait_ge(place, PLACE * B)
            v.tensor_copy(pad_at[:, :], carry[0:1, :]).then_inc(pad_idx, 1)
            dve.wait_ge(made_v, 6 + E)
            link(v.tensor_tensor(count[:, :], carry[0:1, :], region[:, :], ALU.subtract))
            link(v.tensor_copy(count_i[:, :], count[:, :]))
            link(v.tensor_scalar(count_i[:, :], count_i[:, :], TILE.bit_length() - 1, None, ALU.arith_shift_right))
            link(v.tensor_copy(tiles[:, :], count_i[:, :]))
            link(v.tensor_copy(ends[:, 0:1], tiles[:, 0:1]))
            for e in range(1, E):
                link(v.tensor_tensor(ends[:, e:e + 1], ends[:, e - 1:e], tiles[:, e:e + 1], ALU.add))
            wide = [1, NTILE, E]
            link(v.tensor_tensor(past[:, :, :], tile_no[:, :].rearrange("p (j o) -> p j o", o=1).to_broadcast(wide),
                                 ends[:, :].rearrange("p (o e) -> p o e", o=1).to_broadcast(wide), ALU.is_ge))
            v.tensor_reduce(owner[:, :], past[:, :, :], AX.X, ALU.add)
            link(v.tensor_tensor(past_n[:, :, :], past[:, :, :],
                                 tiles[:, :].rearrange("p (o e) -> p o e", o=1).to_broadcast(wide), ALU.mult))
            v.tensor_scalar(base[:, :], owner[:, :], float(REGION), None, ALU.mult)
            link(v.tensor_reduce(begun[:, :], past_n[:, :, :], AX.X, ALU.add))
            link(v.tensor_tensor(step_no[:, :], tile_no[:, :], begun[:, :], ALU.subtract))
            link(v.tensor_tensor(spare[:, :], step_no[:, :], past[:, :, E - 1], ALU.mult))
            v.tensor_tensor(spare[:, :], spare[:, :], begun[:, :], ALU.add)
            v.scalar_tensor_tensor(tile_row[:, :], step_no[:, :], float(TILE), base[:, :], ALU.mult, ALU.add)
            link(v.tensor_scalar(tile_expert[:, 4:4 + NTILE], owner[:, :], float(E - 1), None, ALU.min))
            v.tensor_copy(count[:, :], tiles[:, :]).then_inc(tab, 1)
            for n in range(4):
                link(v.tensor_scalar(land[:, :], spare[:, :], float(3 - n), None, ALU.add))
                link(v.tensor_scalar(land[:, :], land[:, :], 2, 5, ALU.arith_shift_right, ALU.arith_shift_left))
                last = v.tensor_scalar(tile_land[:, n, :], land[:, :], 16, None, ALU.add)
                if n < 3:
                    link(last)
            last.then_inc(landed_set, 1)
            for n in range(2):
                dve.wait_ge(rows_out[n], 96 * (B // 2))
                dve.wait_ge(h1_out[n], 16 * (B // 2))
            dve.wait_ge(b2_in, 16)

            def tile(j, has):
                if has(0):
                    for n in range(3):
                        sl = slice(2 * TILE * n, 2 * TILE * n + 2 * TILE)
                        dve.wait_ge(gelu_done, 3 * j.i + n + 1)
                        wait(dve, tile_done, j.i - 1)
                        v.tensor_copy(g_hi[j.odd][:, sl], gelu[j.odd][:, sl]).then_inc(gelu_hi, 1)
                        dve.wait_ge(gelu_hi, 3 * j.i + n + 1)
                        v.tensor_tensor(g_lo[j.odd][:, sl], gelu[j.odd][:, sl], g_hi[j.odd][:, sl], ALU.subtract).then_inc(gelu_lo, 1)
                if has(-1):
                    t = j + -1
                    e = dve.value_load(tile_expert[0:1, bass.ds(t.i + 4, 1)], min_val=0, max_val=E - 1)
                    dve.wait_ge(tile_done, t.i + 1)
                    wait(dve, weighted, t.i)
                    v.tensor_tensor(with_b2[:, :, :], tile_ps[:, 0:2 * D].rearrange("p (u n) -> p u n", u=2),
                                    b2_rows[:, bass.ds(e, 1), :].to_broadcast([128, 2, D]), ALU.add).then_inc(b2_added, 1)
                    dve.wait_ge(b2_added, t.i + 1)
                    dve.wait_ge(added[t.slot % 4], 32 * t.fours() + 16)
                    for u in range(2):
                        last = v.tensor_scalar(result[t.slot % 4][:, u, :], with_b2[:, u, :],
                                               row_in[t.slot][:, u, YWORDS:TOKEN].bitcast(F32)[:, bass.ds(e, 1)], None,
                                               ALU.mult)
                    last.then_inc(weighted, 1)

            expert_tiles(dve, tile)

        @block.tensor
        def _(pe):
            mm, turn_ = nc.tensor.matmul, nc.tensor.transpose

            def product(dst, pairs):
                for n, (lhs, rhs) in enumerate(pairs):
                    last = mm(dst, lhs, rhs, start=(n == 0), stop=(n == len(pairs) - 1))
                return last

            pe.wait_ge(made, 10)
            pe.wait_ge(tokw_in, 16)
            for n in range(3):
                for k in (2 * n, 2 * n + 1):
                    for c in range(2):
                        last = turn_(bank[n][:, D * (k % 2) + DC * c:D * (k % 2) + DC * c + DC],
                                     tokw_nat[:, c, 128 * k:128 * k + 128], ident[0:DC, 0:DC])
                last.then_inc(tokw_t, 1)
            pe.wait_ge(b1_in, 16)
            turn_(b1_ps[:, 0:E * FC], b1_nat[:, :], ident[0:E * FC, 0:E * FC]).then_inc(b1_t, 1)
            pe.wait_ge(tokw_copied, 3)
            for n in range(NSTEP + 1):
                if n < NSTEP:
                    pe.wait_ge(strip_set, n + 1)
                    if n >= 2:
                        pe.wait_ge(strip_copied_v, n - 1)
                        pe.wait_ge(strip_copied_s, n - 1)
                    for k in range(KC):
                        last = turn_(patch_ps[n % 2][k // 3][:, GR * (k % 3):GR * (k % 3) + GR],
                                     strip[n % 2][:, 128 * k:128 * k + 128],
                                     ident[0:GR, 0:GR])
                    last.then_inc(strip_t, 1)
                if n >= 1:
                    m = n - 1
                    pe.wait_ge(strip_copied_v, m + 1)
                    pe.wait_ge(strip_copied_s, m + 1)
                    wait(pe, tok_biased, m - 1)
                    product(tok_ps[m % 2][0:GR, 0:D],
                            [(patches[m % 2][:, k, :], tokw[:, k, :]) for k in range(KC)]).then_inc(tok_done, 1)

            pe.wait_ge(ones_set, 1)
            pe.wait_ge(made_v, 6 + E)
            pe.wait_ge(consts_in, 16 * NCONST)
            pe.wait_ge(wqk_set, 8)
            pe.wait_ge(b1_copied, 1)

            def probs_values(b, grp, c):
                if c == 0:
                    pe.wait_ge(v_scaled, 3 * b.i + grp + 1)
                    if grp != 1:
                        wait(pe, ctx_copied, 2 * b.i + grp // 2)
                for j in range(4):
                    last = mm(PV[32 * j:32 * j + 32, 0:S], v_over[grp][:, c, j, :],
                              probs[(b.odd + grp) % 2][:, j, c, :],
                              start=(c == 0 and grp != 1), stop=(c == SC - 1 and grp != 0))
                if c == SC - 1:
                    last.then_inc(pv_done, 1)

            def iteration(i, has):
                a, c_, d_, e_ = i + 1, i, i + -1, i + -2
                for t in range(H * SC):
                    h = t // SC
                    if has(0):
                        if t % 18 == 0:
                            pe.wait_ge(stack_in[c_.odd][h // HALF], 144 * c_.turn + 144)
                        wait(pe, exp_done, 36 * c_.i + t - 3)
                        mm(SCORE[t % 4][0:SQ, 0:S], k_stack[c_.odd][:, h, SQ * (t % SC):SQ * (t % SC) + SQ],
                           q_stack[c_.odd][:, h, :], start=True, stop=True).then_inc(scores_made, 1)
                    if t == 2 and has(-2):
                        pe.wait_ge(yt_copied, 2 * e_.i + 2)
                        if not has(-1):
                            pe.wait_ge(place, PLACE * (e_.i - 1) + 2)
                        for c in range(SC):
                            last = product(MC[0:SQ, E * c:E * c + E],
                                           [(y_t[:, n, SQ * c:SQ * c + SQ], router_t[:, n, :]) for n in range(2)])
                        last.then_inc(logits_made, 1)
                    if t in (6, 10, 13) and has(-1):
                        probs_values(d_, 2, (6, 10, 13).index(t))
                    if t in (1, 4) and has(1):
                        n = t // 4
                        pe.wait_ge(xn_set, SC * a.i + SC)
                        if has(0):
                            pe.wait_ge(v_copied, 2 * c_.i + 2 - n)
                        settle(pe, pe_settled)
                        rows_ = (128, ONES)[n]
                        for c in range(SC):
                            last = turn_(MA[n][0:rows_, SQ * c:SQ * c + SQ], xn[:, c, 128 * n:128 * n + rows_],
                                         ident[0:SQ, 0:SQ])
                        last.then_inc(xt_made, 1)
                    if t in (15, 17, 20) and has(-1):
                        c = (15, 17, 20).index(t)
                        pe.wait_ge(ctx_copied, 2 * d_.i + 2)
                        if c and has(0):
                            pe.wait_ge(res_added, 3 * d_.i + c)
                        elif has(-2) and has(0):
                            pe.wait_ge(route, ROUTE * e_.i + 1)
                        product(small_bank(c, has)[0:SQ, 0:D], [(ctx_t[:, n, SQ * c:SQ * c + SQ], wo_sb[:, n, :]) for n in range(2)])\
                            .then_inc(proj_done, 1)
                    if t in (6, 8, 9, 12, 22, 24) and has(1):
                        n, k = divmod((6, 8, 9, 12, 22, 24).index(t), 2)
                        if k == 0:
                            pe.wait_ge(xt_copied, 2 * a.i + 2)
                            if n == 2:
                                pe.wait_ge(qk_rest, 3 * a.i + 1)
                        last = mm(MA[n % 2][:, 0:S],
                                  wqk_sb[0:XK[k], k, :, :, :].rearrange("p w n h -> p (w n h)")[:, 128 * n:128 * n + 128],
                                  xt[0:XK[k], k, :], start=(k == 0), stop=(k == 1))
                        if k == 1:
                            last.then_inc(qk_made, 1)
                    if t in (18, 21, 25) and has(0):
                        probs_values(c_, 0, (18, 21, 25).index(t))
                    if t == 25 and has(-2):
                        pe.wait_ge(route, ROUTE * e_.i + ROUTE)
                        if has(-1) and has(0):
                            pe.wait_ge(res_added, 3 * d_.i + 3)
                        mm(MC[0:SQ, 0:SC * E], before[:, :], either[:, :, :].rearrange("p c e -> p (c e)"),
                           start=True, stop=False)
                        for n in range(1, SC):
                            mm(MC[0:SQ, n * E:SC * E], ones_h[:, 0:SQ],
                               either[:, 0:SC - n, :].rearrange("p c e -> p (c e)"), start=False, stop=False)
                        for n in range(SC):
                            last = mm(MC[:, SC * E:SC * E + E], ones_h[:, :], either[:, n, :], start=False, stop=(n == SC - 1))
                        last.then_inc(rank_made, 1)
                    if t in (27, 29, 32) and has(1):
                        c = (27, 29, 32).index(t)
                        pe.wait_ge(qk_rest, 3 * a.i + 2 + c // 2)
                        last = product(MA[1 - c // 2][0:SQ, D * (c % 2):D * (c % 2) + D],
                                       [(xt[0:XK[k], k, SQ * c:SQ * c + SQ], wv_sb[0:XK[k], k, :]) for k in range(2)])
                        if c:
                            last.then_inc(v_made, 1)
                    if t in (30, 34) and has(0):
                        probs_values(c_, 1, (t - 30) // 4)
                    if t == 0 and has(-1):
                        probs_values(d_, 1, 2)
                    if t in (33, 35) and has(-1):
                        n = (t - 33) // 2
                        pe.wait_ge(y_set, SC * d_.i + SC)
                        pe.wait_ge(res_added, 3 * d_.i + 3)
                        if has(0) and n == 1:
                            pe.wait_ge(yt_copied, 2 * d_.i + 1)
                        elif has(0) and has(-2):
                            pe.wait_ge(place, PLACE * e_.i + 2)
                        for c in range(SC):
                            last = turn_(small_bank(n, has)[0:DC, SQ * c:SQ * c + SQ], y[:, c, DC * n:DC * n + DC], ident[0:SQ, 0:SQ])
                        last.then_inc(yt_made, 1)

            batches(pe, iteration)

            pe.wait_ge(tab, 1)
            chosen = [pe.alloc_register(f"chosen{n}") for n in range(4 + RING)]

            def rows_t(j):
                pe.wait_ge(tile_in[j.slot], 16 * j.turn + 16)
                wait(pe, yt2_copied, j.i)
                ps = rowt_ps[:, :].bitcast(BF16)
                for k in range(3):
                    for u in range(2):
                        last = turn_(ps[:, TILE * k + 128 * u:TILE * k + 128 * u + 128],
                                     row_in[j.slot][:, u, 0:YWORDS].bitcast(BF16)[:, 128 * k:128 * k + 128], ident_h[:, :])
                last.then_inc(yt2_made, 1)

            def tile(j, has):
                if j.slot == 0:
                    known = 4 + RING if has(0) else 4
                    pe.load(chosen[0:known], tile_expert[0:1, bass.ds(j.i, known)])
                if has(0):
                    pe.wait_ge(yt2_copied, j.i + 1)
                    wait(pe, gelu_done, 3 * j.i - 3)
                    e = pe.snap(chosen[4 + j.slot], min_val=0, max_val=E - 1)
                    for f in range(FC):
                        last = product(hid_ps[j.odd][f // 2][:, TILE * (f % 2):TILE * (f % 2) + TILE],
                                       [(w1_parts[:, bass.ds(e, 1), m, 128 * f:128 * f + 128]
                                         .rearrange("p a n -> p (a n)"), row_t[j.odd][:, k, :]) for m, k in W1_TIMES_Y])
                        if f % 2 == 1:
                            last.then_inc(hid_made, 1)
                if has(1):
                    rows_t(j + 1)
                if has(-1):
                    d_ = j + -1
                    pe.wait_ge(gelu_lo, 3 * d_.i + 3)
                    wait(pe, b2_added, d_.i)
                    e = pe.snap(chosen[3 + j.slot], min_val=0, max_val=E - 1)
                    for f in range(FC):
                        whi, wlo = (w[:, bass.ds(e, 1), f, :].rearrange("p a n -> p (a n)") for w in (w2_hi, w2_lo))
                        for k, (g, w) in enumerate(((g_hi, whi), (g_lo, whi), (g_hi, wlo))):
                            for u in range(2):
                                at = TILE * f + 128 * u
                                last = mm(tile_ps[:, D * u:D * u + D], g[d_.odd][:, at:at + 128], w,
                                          start=(f + k + u == 0), stop=(f == FC - 1 and k == 2 and u == 1))
                    last.then_inc(tile_done, 1)

            rows_t(Step(0, 0, RING))
            expert_tiles(pe, tile)


_INS = ["x", "txt", "L0_tok_W", "L0_tok_b", "L0_attn_Wq", "L0_attn_bq", "L0_attn_Wk", "L0_attn_bk", "L0_attn_Wv",
        "L0_attn_bv", "L0_attn_Wo", "L0_attn_bo", "L0_ffn_router_w", "L0_ffn_w1", "L0_ffn_b1", "L0_ffn_w2", "L0_ffn_b2"]


def kernel(**inputs):
    import numpy as _np
    import concourse.bacc as _bacc
    from concourse import mybir as _mybir
    from concourse.bass_utils import run_bass_kernel_spmd as _run

    nc = _bacc.Bacc("TRN2", target_bir_lowering=False, num_devices=1)
    arrays, args = {}, []
    for name in _INS:
        a = _np.ascontiguousarray(inputs[name])
        if name == "L0_tok_W":
            a = a.reshape(a.shape[0], -1)
        arrays[f"in_{name}"] = a
        args.append(nc.dram_tensor(f"in_{name}", a.shape, _mybir.dt.from_np(a.dtype), kind="ExternalInput").ap())
    batches = inputs["x"].shape[0]
    out = nc.dram_tensor("out_rows", (batches * S + TILE, D), _mybir.dt.float32, kind="ExternalOutput").ap()
    fusion_layer(nc, *args, out)
    r = _run(nc, [arrays], core_ids=[0])
    return r.results[0]["out_rows"][:batches * S].reshape(batches, S, D)
```
